# Optimizing a Trainium2 kernel written in Bass

```python
import numpy as np
import jax
import jax.numpy as jnp

def _softmax(x, axis=-1):
    return jax.nn.softmax(x, axis=axis)

def _gelu(x):
    return jax.nn.gelu(x, approximate=True)

def _silu(x):
    return jax.nn.silu(x)

def _sigmoid(x):
    return jax.nn.sigmoid(x)

def _layernorm(x, axis=-1, eps=1e-05):
    m = jnp.mean(x, axis=axis, keepdims=True)
    v = jnp.var(x, axis=axis, keepdims=True)
    return (x - m) / jnp.sqrt(v + eps)

def _scatter_add(tgt, idx, src, axis=0):
    return tgt.at[idx].add(src)

def _segment_sum(src, seg, n):
    return jax.ops.segment_sum(src, seg, n)
kernel_name = 'mk_cond_seq_d1_seqx_r2_49be34'

def setup_inputs(seed: int=0):
    np.random.seed(seed)
    _w = jnp.asarray

    def _rec_inputs():
        import jax
        import jax.numpy as jnp
        _rk = jax.random.key(seed)
        x = -0.0003929 + 0.9999 * jax.random.normal(jax.random.fold_in(_rk, 1), (2, 2048, 512), jnp.float32)
        _lenS = 2048 - jax.random.randint(jax.random.fold_in(_rk, 7), (2,), 0, max(1, 2048 // 4) + 1, jnp.int32)
        _lenS2 = 2048 - jax.random.randint(jax.random.fold_in(_rk, 8), (2,), 0, max(1, 2048 // 4) + 1, jnp.int32)
        cond_1024 = 0.0061147 + 1.02565 * jax.random.normal(jax.random.fold_in(_rk, 11), (2, 512), jnp.float32)
        return (x, cond_1024)
    x, cond_1024 = _rec_inputs()

    def _L0_cond_setup():
        import jax, jax.numpy as jnp
        import numpy as np
        H = 16
        EPS = 1e-05

        def layer_norm(x, g, b):
            mu = jnp.mean(x, axis=-1, keepdims=True)
            var = jnp.var(x, axis=-1, keepdims=True)
            return (x - mu) * jax.lax.rsqrt(var + EPS) * g + b
        key = jax.random.key(seed)
        ks = jax.random.split(key, 8)
        B, T, D, TE = (4, 2048, 512, 512)
        s = 0.02
        return {'x': jax.random.normal(ks[0], (B, T, D), jnp.float32), 'emb': jax.random.normal(ks[1], (B, 1, TE), jnp.float32), 'gate_msa': jax.random.normal(ks[2], (B, 1, D), jnp.float32), 'norm_g': jnp.ones((D,), jnp.float32), 'norm_b': jnp.zeros((D,), jnp.float32), 'Wq': jax.random.normal(ks[3], (D, D), jnp.float32) * s, 'bq': jnp.zeros((D,), jnp.float32), 'Wk': jax.random.normal(ks[4], (D, D), jnp.float32) * s, 'bk': jnp.zeros((D,), jnp.float32), 'Wv': jax.random.normal(ks[5], (D, D), jnp.float32) * s, 'bv': jnp.zeros((D,), jnp.float32), 'emb_W': jax.random.normal(ks[6], (TE, 2 * D), jnp.float32) * s, 'emb_b': jnp.zeros((2 * D,), jnp.float32), 'sn_g': jnp.ones((D,), jnp.float32), 'sn_b': jnp.zeros((D,), jnp.float32), 'out_W': jax.random.normal(ks[7], (D, D), jnp.float32) * s, 'out_b': jnp.zeros((D,), jnp.float32)}
    _L0_cond_all = _L0_cond_setup()
    _L0_cond_in = {k: v for k, v in _L0_cond_all.items() if k in ('norm_g', 'norm_b', 'Wq', 'bq', 'Wk', 'bk', 'Wv', 'bv', 'emb_W', 'emb_b', 'sn_g', 'sn_b', 'out_W', 'out_b')}
    del _L0_cond_all
    return {'x': x, 'cond_1024': cond_1024, 'L0_cond_norm_g': _L0_cond_in['norm_g'], 'L0_cond_norm_b': _L0_cond_in['norm_b'], 'L0_cond_Wq': _L0_cond_in['Wq'], 'L0_cond_bq': _L0_cond_in['bq'], 'L0_cond_Wk': _L0_cond_in['Wk'], 'L0_cond_bk': _L0_cond_in['bk'], 'L0_cond_Wv': _L0_cond_in['Wv'], 'L0_cond_bv': _L0_cond_in['bv'], 'L0_cond_emb_W': _L0_cond_in['emb_W'], 'L0_cond_emb_b': _L0_cond_in['emb_b'], 'L0_cond_sn_g': _L0_cond_in['sn_g'], 'L0_cond_sn_b': _L0_cond_in['sn_b'], 'L0_cond_out_W': _L0_cond_in['out_W'], 'L0_cond_out_b': _L0_cond_in['out_b']}

def reference(x, cond_1024, L0_cond_norm_g, L0_cond_norm_b, L0_cond_Wq, L0_cond_bq, L0_cond_Wk, L0_cond_bk, L0_cond_Wv, L0_cond_bv, L0_cond_emb_W, L0_cond_emb_b, L0_cond_sn_g, L0_cond_sn_b, L0_cond_out_W, L0_cond_out_b):
    import jax
    import jax.numpy as jnp

    def _L0_cond_ref(x, emb, gate_msa, norm_g, norm_b, Wq, bq, Wk, bk, Wv, bv, emb_W, emb_b, sn_g, sn_b, out_W, out_b):
        import jax, jax.numpy as jnp
        import numpy as np
        H = 16
        EPS = 1e-05

        def layer_norm(x, g, b):
            mu = jnp.mean(x, axis=-1, keepdims=True)
            var = jnp.var(x, axis=-1, keepdims=True)
            return (x - mu) * jax.lax.rsqrt(var + EPS) * g + b
        B, T, D = x.shape
        dh = D // H
        xn = layer_norm(x, norm_g, norm_b)
        q = (xn @ Wq + bq).reshape(B, T, H, dh)
        k = (xn @ Wk + bk).reshape(B, T, H, dh)
        v = (xn @ Wv + bv).reshape(B, T, H, dh)
        q = jax.nn.softmax(q, axis=-1)
        k = jax.nn.softmax(k, axis=1)
        ctx = jnp.einsum('bnhd,bnhl->bhdl', k, v)
        y = jnp.einsum('bnhd,bhdl->bnhl', q, ctx).reshape(B, T, D)
        emb_out = jax.nn.silu(emb) @ emb_W + emb_b
        scale, shift = jnp.split(emb_out, 2, axis=-1)
        h = layer_norm(y, sn_g, sn_b) * (1.0 + scale) + shift
        h = jax.nn.silu(h) @ out_W + out_b
        return x + gate_msa * h
    x = _L0_cond_ref(x, cond_1024[:, None, :], cond_1024[:, None, :], L0_cond_norm_g, L0_cond_norm_b, L0_cond_Wq, L0_cond_bq, L0_cond_Wk, L0_cond_bk, L0_cond_Wv, L0_cond_bv, L0_cond_emb_W, L0_cond_emb_b, L0_cond_sn_g, L0_cond_sn_b, L0_cond_out_W, L0_cond_out_b)
    return x

_drawn_inputs = setup_inputs


def setup_inputs(seed=0):
    import zlib

    import numpy as np

    out = dict(_drawn_inputs(seed))
    spreads = {'L0_cond_norm_g': (1.0, 0.6),
     'L0_cond_norm_b': (0.0, 0.1),
     'L0_cond_bq': (0.0, 0.8),
     'L0_cond_bk': (0.0, 0.8),
     'L0_cond_bv': (0.0, 0.1),
     'L0_cond_emb_b': (0.0, 0.1),
     'L0_cond_sn_g': (1.0, 0.2),
     'L0_cond_sn_b': (0.0, 0.272),
     'L0_cond_out_b': (0.0, 0.1)}
    factors = {'L0_cond_Wq': 8.0, 'L0_cond_Wk': 8.0}
    for name, (base, spread) in spreads.items():
        noise = np.random.default_rng([zlib.crc32(name.encode()), seed]).standard_normal(out[name].shape)
        drawn = base * np.exp(spread * noise) if base else spread * noise
        out[name] = jnp.asarray(drawn.astype(out[name].dtype))
    for name, factor in factors.items():
        out[name] = (out[name] * factor).astype(out[name].dtype)
    return out
```

```python
import math
from contextlib import ExitStack

import concourse.bass as bass
from concourse import mybir

F32 = mybir.dt.float32
F16 = mybir.dt.float16
I32 = mybir.dt.int32
ALU = mybir.AluOpType
ACT = mybir.ActivationFunctionType
AX = mybir.AxisListType

P = 128
HEADS = 16
EPS = 1e-5
ROWS = ["norm_g", "norm_b", "bq", "bk", "bv", "sn_g", "sn_b", "out_b"]
Z_SCALE = 256.0
EK_SHIFT = 15 * math.log(2.0)
TOP = 8192.0
EXPONENT = 0x7F800000
GUESS = 0x5F3759DF - (1 << 22) - (1 << 31)
ROOT_STEPS = 11
LOWEST = -3.4028234e38


def linear_attention_block(nc, x, cond, norm_g, norm_b, Wq, bq, Wk, bk, Wv, bv, emb_W, emb_b,
                           sn_g, sn_b, out_W, out_b, out):
    B, T, D = x.shape
    C = D // P
    DH = D // HEADS
    HC = P // DH
    NP = T // (2 * P)
    EC = emb_W.shape[1] // P
    YW = HC * (DH + 1)
    VR = 8 * C
    NR = VR + EC + B * C

    x_v = x.rearrange("b (i p u) c -> (b i) p u c", p=P, u=2)
    out_v = out.rearrange("b (i p u) c -> (b i) p u c", p=P, u=2)

    def chunked(w):
        return w.rearrange("(j p) n -> p j n", p=P)

    def rows(v):
        return v.rearrange("(j p) -> j p", p=P)

    with ExitStack() as ctx:
        def sb(name, shape, dt=F32):
            return ctx.enter_context(nc.sbuf_tensor(name, shape, dt))

        def sem(name):
            return ctx.enter_context(nc.semaphore(name))

        wk = sb("wk", [P, 2, C, D], F16)
        wq = sb("wq", [P, 2, C, D], F16)
        wo = sb("wo", [P, 2, C, D], F16)
        wv = sb("wv", [P, C, D])
        NB = 3 + 4 * B
        wide = sb("wide", [P, NB, D])
        kb_row, qb_row, vb_row = wide[:, 0, :], wide[:, 1, :], wide[:, 2, :]

        def batch_row(kind, b):
            return wide[:, 3 + 4 * b + kind, :]
        MUL, ADD, GOB, GATE = range(4)

        ident = sb("ident", [P, P])
        ident16 = sb("ident16", [P, P], F16)
        ones = sb("ones", [P, P])
        z256 = sb("z256", [P, 1])
        cols = sb("cols", [P, NR])
        prm = sb("prm", [NR, P])
        silu2 = sb("silu2", [P, B * C])
        silu_t = sb("silu_t", [P, B * C])
        emb_c = sb("emb_c", [P, EC, B])
        final_c = sb("final_c", [P, NB, C])
        final_r = sb("final_r", [NB * C, P])
        stat = sb("stat", [P, 3 + B])
        stat_m = sb("stat_m", [3, 1])
        stat_d = sb("stat_d", [3, 3])
        pow2 = sb("pow2", [P, 3 + B])
        top_r = sb("top_r", [P, 3 + B])
        bound = sb("bound", [P, B, 2])
        bound_m = sb("bound_m", [B, 1])
        bound_d = sb("bound_d", [B, B])
        inv_k, inv_q = sb("inv_k", [P, 1]), sb("inv_q", [P, 1])
        inv_o = sb("inv_o", [P, B])

        zh = sb("zh", [P, 2 * NP, D], F16)
        zl = sb("zl", [P, 2 * NP, D], F16)
        zT = sb("zT", [P, 2 * NP, 2, C, P], F16)
        k_all = sb("k_all", [P, NP, 2, D])
        x_in = sb("x_in", [P, 2, 2, D])
        z_sb = sb("z_sb", [P, 2, 2, D])
        bn6 = sb("bn6", [P, 2, 6])
        mv = sb("mv", [P, 2, 2])
        half_v = sb("half_v", [P, 2])
        root = sb("root", [P, 2])
        root_t = sb("root_t", [P, 2])
        acc = sb("acc", [P, 2, D])
        m_col = sb("m_col", [P, C])
        m_diag = sb("m_diag", [P, C, P])
        m_row = m_diag[:, :, :].rearrange("p j c -> p (j c)")
        ek = sb("ek", [P, 2, 2, D])
        ekh = sb("ekh", [P, 2, 2, D], F16)
        ekl = sb("ekl", [P, 2, 2, D], F16)
        r_s = sb("r_s", [P, C])
        ctx_bd = sb("ctx_bd", [P, C, HC, DH + 1])
        q_sb = sb("q_sb", [P, 2, 2, D])
        q_max = sb("q_max", [P, 2, 2 * HEADS])
        eqT = sb("eqT", [P, 2, C, P])
        r_q = sb("r_q", [P, HEADS])
        y_bn6 = sb("y_bn6", [P, 2, 6])
        y_mv = sb("y_mv", [P, 2, 2])
        y_half_v = sb("y_half_v", [P, 2])
        y_root = sb("y_root", [P, 2, 2])
        y_root_t = sb("y_root_t", [P, 2])
        y_nmr = sb("y_nmr", [P, 2, 2])

        gT = ek[:, :, :, :].rearrange("p a u c -> p (a u) c")
        spare = k_all[:, :, :, :].rearrange("p i u c -> p (i u c)")
        PAIR = 2 * D
        y_sb = spare[:, 0:2 * PAIR].rearrange("p (a u c) -> p a u c", a=2, u=2)
        t_sb = spare[:, 2 * PAIR:3 * PAIR].rearrange("p (u c) -> p u c", u=2)
        sT = spare[:, 3 * PAIR:4 * PAIR].bitcast(F16).rearrange("p (s u j c) -> p s u j c", s=2, u=2, j=C)
        fo = spare[:, 4 * PAIR:6 * PAIR].rearrange("p (a u c) -> p a u c", a=2, u=2)
        xr = spare[:, 6 * PAIR:8 * PAIR].rearrange("p (a u c) -> p a u c", a=2, u=2)
        wk_raw, wq_raw, wo_raw = (
            spare[:, n * C * D:(n + 1) * C * D].rearrange("p (j n) -> p j n", j=C) for n in range(3))
        zT_words = zT[:, :, :, :, :].rearrange("p t s j c -> p (t s j c)").bitcast(F32)
        wk_g, wq_g = (zT_words[:, n * C * D:(n + 1) * C * D].rearrange("p (j n) -> p j n", j=C) for n in (2, 3))
        emb_a = ek[:, :, :, :].rearrange("p a u c -> p (a u) c").rearrange("p (j h) c -> p j (h c)", h=2)
        emb_b2 = q_sb[:, :, :, :].rearrange("p a u c -> p (a u) c").rearrange("p (j h) c -> p j (h c)", h=2)

        scratch = nc.dram_tensor("rows_scratch", [NB * C, P], F32, kind="Internal").ap()

        ps = ctx.enter_context(nc.psum_tensor("ps", [P, 8, D], F32))
        ps16 = ps[:, :, :].bitcast(F16)
        Q_BANK, K_BANK, EQT_BANK, Y_BANK, OUT_BANK, ST_BANK = 0, 2, 2, 4, 6, 7
        G_BANK, M_BANK, CTX_BANK = 2, 6, 6

        names = """prm_in x_in_done wk_in wq_in wv_in wo_in emb_in const_ready prm_T cols_ready silu_ready silu2_ready
            emb_done fin_done rowsT rows_copied scr_out wide_in stat_ready statT stat_max_done stat_b
            wk_scaled wq_scaled wk_hi wq_hi wo_hi wk_ready wq_ready wo_ready wv_ready bound_ready boundT
            bound_diag bound_b scales_ready setup_step fin_step
            stat_step z_ready zh_ready zl_ready t_done zT_ready k_done k_ready kmax_done
            kT_done mdiag_ready mrow_done mrow_ready acc_cleared
            ksub_done exp_done ekh_ready ekl_ready s_done g_pair s_sum gT_ready ctx_done ctx_step ctx_ready
            q_done q_evac qmax_done qsub_done qexp_done eqT_done eqT_ready y_done y_ready y_step ystat_ready
            n_ready mul_ready h_ready tanh_ready s_ready sT_done sh_ready sl_ready o_done fin_ready
            xr_in xg_ready out_ready stored rq_step""".split()
        S = {n: sem(n) for n in names}

        block = ctx.enter_context(nc.Block())

        def starts(g, n):
            return isinstance(g, int) and g < n

        def over_pairs(eng, b, peel, end, step):
            first = b * NP
            peeled = peel if b == 0 else 0
            for i in range(peeled):
                step(i, first + i)
            with eng.Fori(peeled, end) as i:
                step(i, i + first)

        @block.sync
        def _(sp):
            for n, v in enumerate([norm_g, norm_b, bq, bk, bv, sn_g, sn_b, out_b]):
                sp.dma_start(prm[n * C:(n + 1) * C, :], rows(v)).then_inc(S["prm_in"], 16)
            sp.dma_start(prm[VR:VR + EC, :], rows(emb_b)).then_inc(S["prm_in"], 16)
            sp.dma_start(prm[VR + EC:NR, :], cond.rearrange("b (j p) -> (b j) p", p=P)).then_inc(S["prm_in"], 16)
            sp.dma_start(wk_raw, chunked(Wk)).then_inc(S["wk_in"], 16)
            sp.dma_start(x_in[:, 0, :, :], x_v[0]).then_inc(S["x_in_done"], 16)
            sp.dma_start(wq_raw, chunked(Wq)).then_inc(S["wq_in"], 16)
            sp.dma_start(wo_raw, chunked(out_W)).then_inc(S["wo_in"], 16)
            sp.wait_ge(S["x_in_done"], 16)
            sp.dma_start(x_in[:, 1, :, :], x_v[1]).then_inc(S["x_in_done"], 16)
            sp.dma_start(wv[:, :, :], chunked(Wv)).then_inc(S["wv_in"], 16)
            sp.dma_start(emb_a, chunked(emb_W)[:, 0:2, :]).then_inc(S["emb_in"], 16)
            sp.dma_start(emb_b2, chunked(emb_W)[:, 2:4, :]).then_inc(S["emb_in"], 16)
            sp.wait_ge(S["rows_copied"], 1)
            sp.dma_start(scratch, final_r[:, :]).then_inc(S["scr_out"], 16)
            sp.wait_ge(S["scr_out"], 16)
            sp.dma_start(wide[:, :, :].rearrange("p n c -> p (n c)"),
                         scratch.rearrange("(o r) c -> o (r c)", o=1).broadcast_to([P, NB * D])
                         ).then_inc(S["wide_in"], 16)

            def load_x(g):
                sp.wait_ge(S["x_in_done"], 16 * g)
                sp.wait_ge(S["z_ready"], g - 1)
                sp.dma_start(x_in[:, g % 2, :, :], x_v[g]).then_inc(S["x_in_done"], 16)

            def load_residual(g):
                if not starts(g, 1):
                    sp.wait_ge(S["xr_in"], 16 * g)
                sp.dma_start(xr[:, g % 2, :, :], x_v[g]).then_inc(S["xr_in"], 16)

            def store(g):
                if not starts(g, 1):
                    sp.wait_ge(S["stored"], 16 * g)
                sp.wait_ge(S["out_ready"], 2 * g + 2)
                sp.dma_start(out_v[g], fo[:, g % 2, :, :]).then_inc(S["stored"], 16)

            for b in range(B):
                first = b * NP
                for i in range(2, NP):
                    load_x(first + i)
                if b + 1 < B:
                    load_x(first + NP)
                    load_x(first + NP + 1)
                sp.wait_ge(S["ksub_done"], first + NP)
                load_residual(first)
                load_residual(first + 1)
                def step(i, g):
                    store(g)
                    load_residual(g + 2)

                over_pairs(sp, b, 1, NP - 2, step)
                store(first + NP - 2)
                store(first + NP - 1)
            sp.wait_ge(S["stored"], 16 * B * NP)

        @block.gpsimd
        def _(pool):
            pool.memset(ident[:, :], 0.0).then_inc(S["const_ready"], 1)
            pool.memset(ones[:, :], 1.0).then_inc(S["const_ready"], 1)
            pool.wait_ge(S["const_ready"], 2)
            pool.affine_select(out=ident[:, :], in_=ident[:, :], compare_op=ALU.not_equal, fill=1.0, base=0,
                               pattern=[[-1, P]], channel_multiplier=1).then_inc(S["const_ready"], 1)
            pool.wait_ge(S["const_ready"], 3)
            pool.tensor_copy(ident16[:, :], ident[:, :]).then_inc(S["const_ready"], 1)

            def low_z(g, i):
                pool.wait_ge(S["zh_ready"], g + 1)
                pool.tensor_tensor(zl[:, bass.ts(i, 2), :], z_sb[:, g % 2, :, :], zh[:, bass.ts(i, 2), :],
                                   ALU.subtract).then_inc(S["zl_ready"], 1)

            def sub_max(g, i):
                if not starts(g, 2):
                    pool.wait_ge(S["s_done"], g - 1)
                    pool.wait_ge(S["ekl_ready"], g - 1)
                pool.tensor_tensor(ek[:, g % 2, :, :], k_all[:, i, :, :],
                                   m_row.rearrange("p (o c) -> p o c", o=1).broadcast_to([P, 2, D]),
                                   ALU.subtract).then_inc(S["ksub_done"], 1)

            def sub_q_max(g):
                pool.wait_ge(S["qmax_done"], g + 1)
                q = q_sb[:, g % 2, :, :].rearrange("p u (h d) -> p (u h) d", d=DH)
                m = q_max[:, g % 2, :].rearrange("p (h o) -> p h o", o=1)
                pool.tensor_tensor(q, q, m.broadcast_to([P, 2 * HEADS, DH]), ALU.subtract).then_inc(S["qsub_done"], 1)

            def modulate(g, b):
                pool.wait_ge(S["n_ready"], 2 * g + 2)
                y = y_sb[:, g % 2, :, :]
                pool.tensor_tensor(y, y, wide[:, 3 + 4 * b + MUL:4 + 4 * b + MUL, :].broadcast_to([P, 2, D]),
                                   ALU.mult).then_inc(S["mul_ready"], 1)

            def residual(g, b):
                pool.wait_ge(S["xr_in"], 16 * g + 16)
                r = xr[:, g % 2, :, :]
                pool.tensor_tensor(r, r, wide[:, 3 + 4 * b + GOB:4 + 4 * b + GOB, :].broadcast_to([P, 2, D]),
                                   ALU.add).then_inc(S["xg_ready"], 1)

            def add_residual(g, u):
                pool.wait_ge(S["fin_ready"], 2 * g + u + 1)
                if u == 0:
                    pool.wait_ge(S["xg_ready"], g + 1)
                pool.tensor_tensor(fo[:, g % 2, u, :], fo[:, g % 2, u, :], xr[:, g % 2, u, :],
                                   ALU.add).then_inc(S["out_ready"], 1)

            for b in range(B):
                first = b * NP
                if b == 0:
                    low_z(0, 0)
                    low_z(1, 1)
                if b > 0:
                    pool.wait_ge(S["s_sum"], b)
                pool.memset(acc[:, :, :], LOWEST).then_inc(S["acc_cleared"], 1)
                with pool.Fori(2, NP) as i:
                    low_z(i + first, i)
                pool.wait_ge(S["kT_done"], b + 1)
                pool.memset(acc[:, :, :], 0.0).then_inc(S["acc_cleared"], 1)
                pool.wait_ge(S["mrow_ready"], b + 1)
                if b > 0:
                    pool.wait_ge(S["ctx_done"], b)
                if b == 0:
                    pool.wait_ge(S["emb_done"], 1)
                sub_max(first, 0)
                sub_max(first + 1, 1)
                with pool.Fori(2, NP) as i:
                    sub_max(i + first, i)
                sub_q_max(first)
                pool.wait_ge(S["wide_in"], 16)
                sub_q_max(first + 1)
                modulate(first, b)
                sub_q_max(first + 2)

                def step(i, g, more_q=True, more_y=True):
                    if more_y:
                        modulate(g + 1, b)
                    residual(g, b)
                    add_residual(g, 0)
                    if more_q:
                        sub_q_max(g + 3)
                    add_residual(g, 1)

                over_pairs(pool, b, 0, NP - 3, step)
                step(NP - 3, first + NP - 3, False, True)
                step(NP - 2, first + NP - 2, False, True)
                if b + 1 < B:
                    low_z(first + NP, 0)
                    low_z(first + NP + 1, 1)
                step(NP - 1, first + NP - 1, False, False)

        @block.scalar
        def _(act):
            act.wait_ge(S["cols_ready"], 1)
            act.activation(silu_t[:, :], cols[:, VR + EC:NR], ACT.Tanh, scale=0.5).then_inc(S["silu_ready"], 1)

            def high_z(g, i):
                act.wait_ge(S["z_ready"], g + 1)
                act.activation(zh[:, bass.ts(i, 2), :], z_sb[:, g % 2, :, :], ACT.Copy).then_inc(S["zh_ready"], 1)

            def keep_zT(g, i, u):
                if u == 0:
                    act.wait_ge(S["t_done"], 2 * g + 2)
                act.activation(zT[:, 2 * i + u, :, :, :].rearrange("p s j c -> p (s j c)"), ps16[:, Q_BANK + u, :],
                               ACT.Copy).then_inc(S["zT_ready"], 1)

            def exp_k(g):
                act.wait_ge(S["ksub_done"], g + 1)
                e = ek[:, g % 2, :, :]
                act.activation(e, e, ACT.Exp).then_inc(S["exp_done"], 1)
                act.wait_ge(S["exp_done"], g + 1)
                if not starts(g, 2):
                    act.wait_ge(S["g_pair"], g - 1)
                act.activation(ekh[:, g % 2, :, :], e, ACT.Copy).then_inc(S["ekh_ready"], 1)

            def exp_q(g):
                act.wait_ge(S["qsub_done"], g + 1)
                q = q_sb[:, g % 2, :, :]
                act.activation(q, q, ACT.Exp).then_inc(S["qexp_done"], 1)

            def keep_eqT(g, u):
                act.wait_ge(S["eqT_done"], 2 * g + u + 1)
                if not starts(g, 1):
                    act.wait_ge(S["y_done"], 2 * g + u - 1)
                act.activation(eqT[:, u, :, :].rearrange("p j c -> p (j c)"), ps[:, EQT_BANK + u, :],
                               ACT.Copy).then_inc(S["eqT_ready"], 1)

            def normalise(g, u):
                act.wait_ge(S["ystat_ready"], g + 1)
                y = y_sb[:, g % 2, u, :]
                act.activation(y, y, ACT.Identity, bias=y_nmr[:, g % 2, u:u + 1],
                               scale=y_root[:, g % 2, u:u + 1]).then_inc(S["n_ready"], 1)

            def tanh_h(g):
                act.wait_ge(S["cols_ready"], 1)
                act.wait_ge(S["h_ready"], g + 1)
                if not starts(g, 1):
                    act.wait_ge(S["s_ready"], g)
                act.activation(t_sb, y_sb[:, g % 2, :, :], ACT.Tanh, scale=0.5).then_inc(S["tanh_ready"], 1)

            def high_s(g, u, b):
                act.wait_ge(S["sT_done"], 2 * g + u + 1)
                if not starts(g, 1):
                    act.wait_ge(S["o_done"], 2 * g + u - 1)
                act.activation(sT[:, 0, u, :, :].rearrange("p j c -> p (j c)"), ps[:, ST_BANK, :], ACT.Identity,
                               scale=top_r[:, 3 + b:4 + b]).then_inc(S["sh_ready"], 1)

            def split_high(w, raw, n, ready):
                act.activation(w[:, 0, :, :], raw, ACT.Identity, scale=top_r[:, n:n + 1]).then_inc(ready, 1)

            high_z(0, 0)
            act.wait_ge(S["scales_ready"], 1)
            split_high(wk, wk_g, 0, S["wk_hi"])
            split_high(wq, wq_g, 1, S["wq_hi"])
            split_high(wo, wo_raw, 2, S["wo_hi"])
            high_z(1, 1)
            keep_zT(0, 0, 0)
            keep_zT(0, 0, 1)
            for b in range(B):
                first = b * NP
                with act.Fori(0, NP - 2) as i:
                    keep_zT(i + (first + 1), i + 1, 0)
                    keep_zT(i + (first + 1), i + 1, 1)
                    high_z(i + (first + 2), i + 2)
                keep_zT(first + NP - 1, NP - 1, 0)
                keep_zT(first + NP - 1, NP - 1, 1)
                exp_k(first)
                exp_k(first + 1)
                with act.Fori(2, NP) as i:
                    exp_k(i + first)
                exp_q(first)
                act.wait_ge(S["g_pair"], first + NP)
                act.activation(gT[:, 0:2, :], ps[:, G_BANK:G_BANK + 2, :], ACT.Copy).then_inc(S["gT_ready"], 1)
                keep_eqT(first, 0)
                keep_eqT(first, 1)
                normalise(first, 0)
                normalise(first, 1)
                exp_q(first + 1)
                keep_eqT(first + 1, 0)
                keep_eqT(first + 1, 1)
                tanh_h(first)

                def step(i, g, more_y=True, more_n=True):
                    high_s(g, 0, b)
                    if more_y:
                        exp_q(g + 2)
                    if more_n:
                        normalise(g + 1, 0)
                        normalise(g + 1, 1)
                    if more_y:
                        keep_eqT(g + 2, 0)
                        keep_eqT(g + 2, 1)
                    high_s(g, 1, b)
                    if more_n:
                        tanh_h(g + 1)

                over_pairs(act, b, 1, NP - 3, step)
                step(NP - 3, first + NP - 3, True, True)
                step(NP - 2, first + NP - 2, False, True)
                if b + 1 < B:
                    high_z(first + NP, 0)
                    high_z(first + NP + 1, 1)
                step(NP - 1, first + NP - 1, False, False)
                if b + 1 < B:
                    keep_zT(first + NP, 0, 0)
                    keep_zT(first + NP, 0, 1)

        @block.vector
        def _(dve):
            def inverse_root(step, at, var, scale, half, y, tmp):
                dve.tensor_scalar(half, var, EPS, 0.5 * scale, ALU.add, ALU.mult).then_inc(step, 1)
                dve.wait_ge(step, at + 1)
                dve.tensor_scalar(y.bitcast(I32), half.bitcast(I32), -0.5, float(GUESS), ALU.mult, ALU.add).then_inc(step, 1)
                dve.wait_ge(step, at + 2)
                for n in range(3):
                    dve.tensor_tensor(tmp, y, y, ALU.mult).then_inc(step, 1)
                    dve.wait_ge(step, at + 3 * n + 3)
                    dve.tensor_tensor(tmp, tmp, half, ALU.mult).then_inc(step, 1)
                    dve.wait_ge(step, at + 3 * n + 4)
                    dve.scalar_tensor_tensor(out=y, in0=tmp, scalar=-1.5, in1=y, op0=ALU.add,
                                             op1=ALU.mult).then_inc(step, 1)
                    dve.wait_ge(step, at + 3 * n + 5)

            def front(g):
                at = (4 + ROOT_STEPS) * g
                step = S["stat_step"]
                dve.wait_ge(S["x_in_done"], 16 * g + 16)
                for u in range(2):
                    dve.bn_stats(bn6[:, u, :], x_in[:, g % 2, u, :]).then_inc(step, 1)
                dve.wait_ge(step, at + 2)
                dve.memset(root_t[:, :], 0.0)
                for u in range(2):
                    dve.bn_aggr(mv[:, u, :], bn6[:, u, :]).then_inc(step, 1)
                dve.wait_ge(step, at + 4)
                inverse_root(step, at + 4, mv[:, :, 1], 1.0 / Z_SCALE ** 2, half_v[:, :], root[:, :], root_t[:, :])
                if not starts(g, 2):
                    dve.wait_ge(S["zl_ready"], g - 1)
                dve.tensor_scalar(z_sb[:, g % 2, 0, :], x_in[:, g % 2, 0, :], mv[:, 0, 0:1], root[:, 0:1],
                                  ALU.subtract, ALU.mult)
                dve.tensor_scalar(z_sb[:, g % 2, 1, :], x_in[:, g % 2, 1, :], mv[:, 1, 0:1], root[:, 1:2],
                                  ALU.subtract, ALU.mult).then_inc(S["z_ready"], 1)

            def keep_k(g, i):
                bank = K_BANK + 2 * (g % 2)
                dve.wait_ge(S["k_done"], 2 * g + 2)
                dve.scalar_tensor_tensor(out=k_all[:, i, :, :], in0=ps[:, bass.ds(bank, 2), :], scalar=inv_k[:, 0:1],
                                         in1=wide[:, 0:1, :].broadcast_to([P, 2, D]), op0=ALU.mult,
                                         op1=ALU.add).then_inc(S["k_ready"], 1)

            def running_max(g, i):
                dve.wait_ge(S["k_ready"], g + 1)
                dve.tensor_tensor(acc[:, :, :], acc[:, :, :], k_all[:, i, :, :], ALU.max).then_inc(S["kmax_done"], 1)
                dve.wait_ge(S["kmax_done"], g + 1)

            def split_ek(g):
                dve.wait_ge(S["exp_done"], g + 1)
                dve.tensor_tensor(acc[:, :, :], acc[:, :, :], ek[:, g % 2, :, :], ALU.add).then_inc(S["s_done"], 1)
                dve.wait_ge(S["ekh_ready"], g + 1)
                if not starts(g, 2):
                    dve.wait_ge(S["g_pair"], g - 1)
                dve.tensor_tensor(ekl[:, g % 2, :, :], ek[:, g % 2, :, :], ekh[:, g % 2, :, :],
                                  ALU.subtract).then_inc(S["ekl_ready"], 1)
                dve.wait_ge(S["s_done"], g + 1)

            def keep_q(g):
                dve.wait_ge(S["q_done"], 2 * g + 2)
                if not starts(g, 2):
                    dve.wait_ge(S["eqT_done"], 2 * g - 2)
                dve.scalar_tensor_tensor(out=q_sb[:, g % 2, :, :], in0=ps[:, Q_BANK:Q_BANK + 2, :],
                                         scalar=inv_q[:, 0:1], in1=wide[:, 1:2, :].broadcast_to([P, 2, D]),
                                         op0=ALU.mult, op1=ALU.add).then_inc(S["q_evac"], 1)

            def max_q(g):
                dve.wait_ge(S["q_evac"], g + 1)
                dve.tensor_reduce(q_max[:, g % 2, :], q_sb[:, g % 2, :, :].rearrange("p u (h d) -> p (u h) d", d=DH),
                                  AX.X, ALU.max).then_inc(S["qmax_done"], 1)

            def keep_y(g, u):
                dve.wait_ge(S["y_done"], 2 * g + u + 1)
                both = ps[:, Y_BANK:Y_BANK + 2, 0:2 * YW].rearrange("p a (h d) -> p a h d", d=DH + 1)
                dve.reciprocal(r_q[:, :].rearrange("p (a h o) -> p a h o", a=2, o=1),
                               both[:, :, :, DH:DH + 1]).then_inc(S["rq_step"], 1)
                dve.wait_ge(S["rq_step"], 2 * g + u + 1)
                if u == 0 and not starts(g, 2):
                    dve.wait_ge(S["sT_done"], 2 * g - 2)
                dve.tensor_tensor(y_sb[:, g % 2, u, :].rearrange("p (a h d) -> p a h d", a=2, d=DH),
                                  both[:, :, :, 0:DH],
                                  r_q[:, :].rearrange("p (a h o) -> p a h o", a=2, o=1)
                                  .broadcast_to([P, 2, HEADS // 2, DH]), ALU.mult).then_inc(S["y_ready"], 1)

            def stats_y(g):
                at = (4 + ROOT_STEPS) * g
                step = S["y_step"]
                dve.wait_ge(S["y_ready"], 2 * g + 2)
                for u in range(2):
                    dve.bn_stats(y_bn6[:, u, :], y_sb[:, g % 2, u, :]).then_inc(step, 1)
                dve.wait_ge(step, at + 2)
                dve.memset(y_root_t[:, :], 0.0)
                for u in range(2):
                    dve.bn_aggr(y_mv[:, u, :], y_bn6[:, u, :]).then_inc(step, 1)
                dve.wait_ge(step, at + 4)
                inverse_root(step, at + 4, y_mv[:, :, 1], 1.0, y_half_v[:, :], y_root[:, g % 2, :], y_root_t[:, :])
                dve.scalar_tensor_tensor(out=y_nmr[:, g % 2, :], in0=y_mv[:, :, 0], scalar=-1.0,
                                         in1=y_root[:, g % 2, :], op0=ALU.mult,
                                         op1=ALU.mult).then_inc(S["ystat_ready"], 1)

            def shift_h(g, b):
                dve.wait_ge(S["mul_ready"], g + 1)
                y = y_sb[:, g % 2, :, :]
                dve.tensor_tensor(y, y, wide[:, 3 + 4 * b + ADD:4 + 4 * b + ADD, :].broadcast_to([P, 2, D]),
                                  ALU.add).then_inc(S["h_ready"], 1)

            def silu_h(g):
                dve.wait_ge(S["tanh_ready"], g + 1)
                y = y_sb[:, g % 2, :, :]
                dve.scalar_tensor_tensor(out=y, in0=t_sb, scalar=1.0, in1=y, op0=ALU.add,
                                         op1=ALU.mult).then_inc(S["s_ready"], 1)

            def low_s(g, u, b):
                dve.wait_ge(S["sh_ready"], 2 * g + u + 1)
                dve.scalar_tensor_tensor(out=sT[:, 1, u, :, :].rearrange("p j c -> p (j c)"), in0=ps[:, ST_BANK, :],
                                         scalar=top_r[:, 3 + b:4 + b],
                                         in1=sT[:, 0, u, :, :].rearrange("p j c -> p (j c)"), op0=ALU.mult,
                                         op1=ALU.subtract).then_inc(S["sl_ready"], 1)

            def keep_out(g, u, b):
                dve.wait_ge(S["o_done"], 2 * g + u + 1)
                if u == 0 and not starts(g, 2):
                    dve.wait_ge(S["stored"], 16 * g - 16)
                dve.scalar_tensor_tensor(out=fo[:, g % 2, u, :], in0=ps[:, OUT_BANK, :], scalar=inv_o[:, b:b + 1],
                                         in1=batch_row(GATE, b), op0=ALU.mult,
                                         op1=ALU.mult).then_inc(S["fin_ready"], 1)

            done = [0]

            def link(ins):
                done[0] += 1
                ins.then_inc(S["setup_step"], 1)
                dve.wait_ge(S["setup_step"], done[0])

            dve.wait_ge(S["prm_T"], 1)
            dve.tensor_copy(cols[:, :], ps[:, 7, 0:NR]).then_inc(S["cols_ready"], 1)
            dve.wait_ge(S["cols_ready"], 1)
            dve.wait_ge(S["wk_in"], 16)
            for j in range(C):
                last = dve.tensor_scalar(wk_g[:, j, :], wk_raw[:, j, :], cols[:, j:j + 1], None, ALU.mult)
            link(last)
            dve.tensor_reduce(stat[:, 0:1], wk_g, AX.XY, ALU.max, apply_absolute_value=True)
            dve.wait_ge(S["wq_in"], 16)
            for j in range(C):
                last = dve.tensor_scalar(wq_g[:, j, :], wq_raw[:, j, :], cols[:, j:j + 1], None, ALU.mult)
            link(last)
            dve.tensor_reduce(stat[:, 1:2], wq_g, AX.XY, ALU.max, apply_absolute_value=True)
            dve.wait_ge(S["wo_in"], 16)
            dve.tensor_reduce(stat[:, 2:3], wo_raw, AX.XY, ALU.max, apply_absolute_value=True).then_inc(S["stat_ready"], 1)

            def spread_max(n, turned, m, d, ready):
                link(dve.tensor_reduce(m[:, :], turned, AX.X, ALU.max))
                dve.tensor_scalar(d[:, :], ident[0:n, 0:n], m[:, 0:1], None, ALU.mult).then_inc(ready, 1)

            def to_power(src, a, z):
                link(dve.tensor_scalar(pow2[:, a:z], src, 1e-30, None, ALU.max))
                link(dve.tensor_scalar(pow2[:, a:z].bitcast(I32), pow2[:, a:z].bitcast(I32), EXPONENT, None,
                                       ALU.bitwise_and))
                link(dve.reciprocal(top_r[:, a:z], pow2[:, a:z]))
                link(dve.tensor_scalar(top_r[:, a:z], top_r[:, a:z], TOP, None, ALU.mult))

            dve.wait_ge(S["statT"], 1)
            spread_max(3, ps[0:3, 6, 0:P], stat_m, stat_d, S["stat_max_done"])
            dve.wait_ge(S["stat_b"], 1)
            to_power(ps[:, 6, 0:3], 0, 3)
            dve.tensor_scalar(inv_k[:, :], pow2[:, 0:1], 1.0 / (TOP * Z_SCALE), None, ALU.mult)
            dve.tensor_scalar(inv_q[:, :], pow2[:, 1:2], 1.0 / (TOP * Z_SCALE), None, ALU.mult).then_inc(S["scales_ready"], 1)

            def split_low(w, raw, n, high, ready):
                dve.wait_ge(high, 1)
                dve.scalar_tensor_tensor(out=w[:, 1, :, :], in0=raw, scalar=top_r[:, n:n + 1], in1=w[:, 0, :, :],
                                         op0=ALU.mult, op1=ALU.subtract).then_inc(ready, 1)

            front(0)
            split_low(wk, wk_g, 0, S["wk_hi"], S["wk_ready"])
            front(1)
            split_low(wq, wq_g, 1, S["wq_hi"], S["wq_ready"])
            split_low(wo, wo_raw, 2, S["wo_hi"], S["wo_ready"])
            dve.wait_ge(S["silu_ready"], 1)
            dve.scalar_tensor_tensor(out=silu2[:, :], in0=silu_t[:, :], scalar=1.0, in1=cols[:, VR + EC:NR],
                                     op0=ALU.add, op1=ALU.mult).then_inc(S["silu2_ready"], 1)
            dve.wait_ge(S["emb_done"], 1)
            for j in range(C):
                last = dve.tensor_scalar(wv[:, j, :], wv[:, j, :], cols[:, j:j + 1], None, ALU.mult)
            last.then_inc(S["wv_ready"], 1)
            pc = ps[:, 7, :]
            link(dve.scalar_tensor_tensor(out=emb_c[:, :, :], in0=pc[:, 0:EC * B].rearrange("p (o b) -> p o b", b=B),
                                     scalar=0.5, in1=cols[:, VR:VR + EC].rearrange("p (o b) -> p o b", b=1)
                                     .broadcast_to([P, EC, B]), op0=ALU.mult, op1=ALU.add))
            for n, r in enumerate((3, 2, 4)):
                link(dve.tensor_tensor(final_c[:, n, :], pc[:, EC * B + n * C:EC * B + (n + 1) * C],
                                       cols[:, r * C:(r + 1) * C], ALU.add))
            sng, snb, ob = cols[:, 5 * C:6 * C], cols[:, 6 * C:7 * C], cols[:, 7 * C:8 * C]
            for b in range(B):
                scale, shift = emb_c[:, 0:C, b], emb_c[:, C:2 * C, b]
                gate = cols[:, VR + EC + b * C:VR + EC + (b + 1) * C]
                f = 3 + 4 * b
                link(dve.scalar_tensor_tensor(out=final_c[:, f + MUL, :], in0=scale, scalar=1.0, in1=sng,
                                              op0=ALU.add, op1=ALU.mult))
                link(dve.scalar_tensor_tensor(out=final_c[:, f + ADD, :], in0=scale, scalar=1.0, in1=snb,
                                              op0=ALU.add, op1=ALU.mult))
                link(dve.tensor_tensor(final_c[:, f + ADD, :], final_c[:, f + ADD, :], shift, ALU.add))
                link(dve.tensor_tensor(final_c[:, f + GOB, :], gate, ob, ALU.mult))
                link(dve.tensor_copy(final_c[:, f + GATE, :], gate))
                link(dve.tensor_reduce(bound[:, b, :], final_c[:, f:f + 2, :], AX.X, ALU.max,
                                       apply_absolute_value=True))
                dve.scalar_tensor_tensor(out=stat[:, 3 + b:4 + b], in0=bound[:, b, 0:1], scalar=math.sqrt(D) * 1.01,
                                         in1=bound[:, b, 1:2], op0=ALU.mult, op1=ALU.add).then_inc(S["bound_ready"], 1)
            dve.wait_ge(S["rowsT"], 1)
            dve.tensor_copy(final_r[:, :], ps[0:NB * C, 7, 0:P]).then_inc(S["rows_copied"], 1)
            dve.wait_ge(S["boundT"], 1)
            spread_max(B, ps[0:B, 6, 0:P], bound_m, bound_d, S["bound_diag"])
            dve.wait_ge(S["bound_b"], 1)
            to_power(ps[:, 6, 0:B], 3, 3 + B)
            for b in range(B):
                link(dve.scalar_tensor_tensor(out=inv_o[:, b:b + 1], in0=pow2[:, 3 + b:4 + b], scalar=0.5 / TOP ** 2,
                                              in1=pow2[:, 2:3], op0=ALU.mult, op1=ALU.mult))
            link(dve.memset(ctx_bd[:, :, :, :], 0.0))
            for r in range(HC):
                last = dve.memset(ctx_bd[r * DH:(r + 1) * DH, :, r, DH:DH + 1], 1.0)
            link(last)
            link(dve.memset(z256[:, :], Z_SCALE))
            dve.wait_ge(S["wide_in"], 16)

            for b in range(B):
                first = b * NP
                if b > 0:
                    dve.wait_ge(S["stored"], 16 * first)
                dve.wait_ge(S["acc_cleared"], 2 * b + 1)
                with dve.Fori(0, NP - 2) as i:
                    front(i + (first + 2))
                    keep_k(i + first, i)
                    running_max(i + first, i)
                for i in range(NP - 2, NP):
                    keep_k(first + i, i)
                    running_max(first + i, i)
                dve.wait_ge(S["kT_done"], b + 1)
                dve.tensor_reduce(m_col[:, :], ps[:, M_BANK:M_BANK + 2, :].rearrange("p u (j t) -> p j u t", j=C),
                                  AX.XY, ALU.max).then_inc(S["ctx_step"], 1)
                dve.wait_ge(S["ctx_step"], 6 * b + 1)
                dve.tensor_tensor(m_diag[:, :, :], ident[:, :].rearrange("p (o c) -> p o c", o=1).broadcast_to([P, C, P]),
                                  m_col[:, :].rearrange("p (j o) -> p j o", o=1).broadcast_to([P, C, P]),
                                  ALU.mult).then_inc(S["mdiag_ready"], 1)
                dve.wait_ge(S["mrow_done"], b + 1)
                dve.tensor_scalar(m_row, ps[:, M_BANK, :], EK_SHIFT, None, ALU.subtract).then_inc(S["mrow_ready"], 1)
                dve.wait_ge(S["acc_cleared"], 2 * b + 2)
                split_ek(first)
                split_ek(first + 1)
                with dve.Fori(2, NP) as i:
                    split_ek(i + first)
                keep_q(first)
                max_q(first)
                dve.wait_ge(S["g_pair"], first + NP)
                dve.tensor_copy(gT[:, 2:4, :], ps[:, G_BANK + 2:G_BANK + 4, :]).then_inc(S["gT_ready"], 1)
                dve.wait_ge(S["s_sum"], b + 1)
                dve.reciprocal(r_s[:, :], ps[:, CTX_BANK + 1, 0:C]).then_inc(S["ctx_step"], 1)
                dve.wait_ge(S["ctx_step"], 6 * b + 2)
                dve.wait_ge(S["ctx_done"], b + 1)
                for r in range(HC):
                    q = slice(r * DH, (r + 1) * DH)
                    last = dve.tensor_tensor(
                        ctx_bd[q, :, r, 0:DH], ps[q, CTX_BANK, :].rearrange("p (j c) -> p j c", j=C)[:, :, q],
                        r_s[q, :].rearrange("p (j o) -> p j o", o=1).broadcast_to([DH, C, DH]), ALU.mult)
                    last.then_inc(S["ctx_step"], 1)
                dve.wait_ge(S["ctx_step"], 6 * b + 6)
                for r in range(HC):
                    q = slice(r * DH, (r + 1) * DH)
                    last = dve.tensor_tensor(
                        ctx_bd[q, :, r, 0:DH], ctx_bd[q, :, r, 0:DH],
                        wide[q, 2, :].rearrange("p (j c) -> p j c", j=C)[:, :, q], ALU.add)
                    last.then_inc(S["ctx_ready"], 1)
                keep_q(first + 1)
                keep_y(first, 0)
                keep_y(first, 1)
                stats_y(first)
                max_q(first + 1)
                keep_q(first + 2)
                max_q(first + 2)
                keep_y(first + 1, 0)
                shift_h(first, b)
                keep_y(first + 1, 1)
                silu_h(first)

                def step(i, g, more_q=True, more_y=True, more_n=True):
                    low_s(g, 0, b)
                    if more_n:
                        stats_y(g + 1)
                    keep_out(g, 0, b)
                    low_s(g, 1, b)
                    if more_n:
                        shift_h(g + 1, b)
                    if more_q:
                        keep_q(g + 3)
                        max_q(g + 3)
                    if more_y:
                        keep_y(g + 2, 0)
                    if more_n:
                        silu_h(g + 1)
                    keep_out(g, 1, b)
                    if more_y:
                        keep_y(g + 2, 1)

                over_pairs(dve, b, 2, NP - 3, step)
                step(NP - 3, first + NP - 3, False, True, True)
                step(NP - 2, first + NP - 2, False, False, True)
                if b + 1 < B:
                    front(first + NP)
                    front(first + NP + 1)
                step(NP - 1, first + NP - 1, False, False, False)

        @block.tensor
        def _(pe):
            def three(out_ap, high, low, w, ready=None):
                n = 0
                for s, part in ((0, high), (1, high), (0, low)):
                    for j in range(C):
                        last = pe.matmul(out_ap, part(j), w[:, s, j, :], start=(n == 0), stop=(n == 3 * C - 1))
                        n += 1
                last.then_inc(ready, 1)

            def turn_z(g, i):
                pe.wait_ge(S["zl_ready"], g + 1)
                for u in range(2):
                    for s, z in enumerate((zh, zl)):
                        for j in range(C):
                            last = pe.transpose(ps16[:, Q_BANK + u, (s * C + j) * P:(s * C + j + 1) * P],
                                                z[:, 2 * i + u, j * P:(j + 1) * P], ident16[:, :])
                    last.then_inc(S["t_done"], 1)

            def product_k(g, i, u):
                pe.wait_ge(S["zT_ready"], 2 * g + u + 1)
                if u == 0 and not starts(g, 2):
                    pe.wait_ge(S["k_ready"], g - 1)
                bank = K_BANK + 2 * (g % 2) + u
                three(ps[:, bank, :], lambda j: zT[:, 2 * i + u, 0, j, :], lambda j: zT[:, 2 * i + u, 1, j, :], wk,
                      S["k_done"])

            def product_q(g, i, u):
                if u == 0 and not starts(g, 1):
                    pe.wait_ge(S["q_evac"], g)
                three(ps[:, Q_BANK + u, :], lambda j: zT[:, 2 * i + u, 0, j, :], lambda j: zT[:, 2 * i + u, 1, j, :],
                      wq, S["q_done"])

            def product_g(g, i, start, stop):
                pe.wait_ge(S["ekl_ready"], g + 1)
                for u in range(2):
                    for c in range(C):
                        for n, (z, e) in enumerate(((zh, ekh), (zh, ekl), (zl, ekh))):
                            last = pe.matmul(ps[:, G_BANK + c, :], z[:, 2 * i + u, c * P:(c + 1) * P],
                                             e[:, g % 2, u, :], start=start and u == 0 and n == 0,
                                             stop=stop and u == 1 and n == 2)
                last.then_inc(S["g_pair"], 1)
                return last

            def turn_q(g, a, u):
                pe.wait_ge(S["qexp_done"], g + 1)
                if not starts(g, 1):
                    pe.wait_ge(S["eqT_ready"], 2 * g + u - 1)
                for j in range(C):
                    last = pe.transpose(ps[:, EQT_BANK + u, j * P:(j + 1) * P], q_sb[:, a, u, j * P:(j + 1) * P],
                                        ident[:, :])
                last.then_inc(S["eqT_done"], 1)

            def product_y(g, u):
                pe.wait_ge(S["eqT_ready"], 2 * g + u + 1)
                if not (starts(g, 1) and u == 0):
                    pe.wait_ge(S["y_ready"], 2 * g + u)
                for j in range(C):
                    last = pe.matmul(ps[:, Y_BANK + j // 2, (j % 2) * YW:(j % 2 + 1) * YW], eqT[:, u, j, :],
                                     ctx_bd[:, j, :, :].rearrange("p h d -> p (h d)"), start=True, stop=True)
                last.then_inc(S["y_done"], 1)

            def turn_s(g, a, u):
                if u == 0:
                    pe.wait_ge(S["s_ready"], g + 1)
                if not (starts(g, 1) and u == 0):
                    pe.wait_ge(S["sl_ready"], 2 * g + u)
                for j in range(C):
                    last = pe.transpose(ps[:, ST_BANK, j * P:(j + 1) * P], y_sb[:, a, u, j * P:(j + 1) * P],
                                        ident[:, :])
                last.then_inc(S["sT_done"], 1)

            def product_out(g, u):
                pe.wait_ge(S["sl_ready"], 2 * g + u + 1)
                if not (starts(g, 1) and u == 0):
                    pe.wait_ge(S["fin_ready"], 2 * g + u)
                three(ps[:, OUT_BANK, :], lambda j: sT[:, 0, u, j, :], lambda j: sT[:, 1, u, j, :], wo, S["o_done"])

            pe.wait_ge(S["const_ready"], 4)
            pe.wait_ge(S["prm_in"], 160)
            pe.transpose(ps[:, 7, 0:NR], prm[:, :], ident[0:NR, 0:NR]).then_inc(S["prm_T"], 1)
            pe.wait_ge(S["stat_ready"], 1)
            pe.transpose(ps[0:3, 6, 0:P], stat[:, 0:3], ident[:, :]).then_inc(S["statT"], 1)
            pe.wait_ge(S["stat_max_done"], 1)
            pe.matmul(ps[:, 6, 0:3], ones[0:3, :], stat_d[:, :], start=True, stop=True).then_inc(S["stat_b"], 1)
            pe.wait_ge(S["cols_ready"], 1)
            pe.wait_ge(S["silu2_ready"], 1)
            pe.wait_ge(S["emb_in"], 32)
            for o in range(EC):
                for j in range(C):
                    e = emb_a if j < 2 else emb_b2
                    pe.matmul(ps[:, 7, o * B:(o + 1) * B], e[:, j % 2, o * P:(o + 1) * P], silu2[:, j:B * C:C],
                              start=(j == 0), stop=(j == C - 1))
            pe.wait_ge(S["wk_in"], 16)
            pe.wait_ge(S["wq_in"], 16)
            pe.wait_ge(S["wv_in"], 16)
            for n, w in enumerate((wk_raw, wq_raw, wv)):
                for o in range(C):
                    at = EC * B + n * C + o
                    for j in range(C):
                        last = pe.matmul(ps[:, 7, at:at + 1], w[:, j, o * P:(o + 1) * P],
                                         cols[:, C + j:C + j + 1], start=(j == 0), stop=(j == C - 1))
            last.then_inc(S["emb_done"], 1)
            pe.wait_ge(S["bound_ready"], B)
            pe.transpose(ps[0:NB * C, 7, 0:P], final_c[:, :, :].rearrange("p n j -> p (n j)"),
                         ident[:, :]).then_inc(S["rowsT"], 1)
            pe.transpose(ps[0:B, 6, 0:P], stat[:, 3:3 + B], ident[:, :]).then_inc(S["boundT"], 1)
            pe.wait_ge(S["bound_diag"], 1)
            pe.matmul(ps[:, 6, 0:B], ones[0:B, :], bound_d[:, :], start=True, stop=True).then_inc(S["bound_b"], 1)
            turn_z(0, 0)
            pe.wait_ge(S["wk_ready"], 1)

            for b in range(B):
                first = b * NP
                def step_a(i, g, more=True):
                    product_k(g, i, 0)
                    if more:
                        pe.wait_ge(S["zT_ready"], 2 * g + 2)
                        turn_z(g + 1, i + 1)
                    product_k(g, i, 1)

                over_pairs(pe, b, 2, NP - 1, step_a)
                step_a(NP - 1, first + NP - 1, False)
                if b == 0:
                    pe.wait_ge(S["wq_ready"], 1)
                pe.wait_ge(S["zT_ready"], 2 * (first + NP))
                product_q(first, 0, 0)
                pe.wait_ge(S["kmax_done"], first + NP)
                for u in range(2):
                    for j in range(C):
                        last = pe.transpose(ps[:, M_BANK + u, j * P:(j + 1) * P], acc[:, u, j * P:(j + 1) * P],
                                            ident[:, :])
                last.then_inc(S["kT_done"], 1)
                product_q(first, 0, 1)
                pe.wait_ge(S["mdiag_ready"], b + 1)
                pe.matmul(ps[:, M_BANK, :], ones[:, :], m_diag[:, :, :].rearrange("p j c -> p (j c)"), start=True,
                          stop=True).then_inc(S["mrow_done"], 1)
                pe.wait_ge(S["k_ready"], first + NP)
                product_g(first, 0, True, False)
                with pe.Fori(1, NP - 1) as i:
                    product_g(i + first, i, False, False)
                product_g(first + NP - 1, NP - 1, False, True)
                pe.wait_ge(S["s_done"], first + NP)
                for j in range(C):
                    for u in range(2):
                        last = pe.matmul(ps[:, CTX_BANK + 1, j:j + 1], acc[:, u, j * P:(j + 1) * P], z256[:, :],
                                         start=(u == 0), stop=(u == 1))
                last.then_inc(S["s_sum"], 1)
                product_q(first + 1, 1, 0)
                pe.wait_ge(S["gT_ready"], 2 * b + 2)
                for j in range(C):
                    for c in range(C):
                        last = pe.matmul(ps[:, CTX_BANK, j * P:(j + 1) * P], gT[:, c, j * P:(j + 1) * P],
                                         wv[:, c, j * P:(j + 1) * P], start=(c == 0), stop=(c == C - 1))
                last.then_inc(S["ctx_done"], 1)
                product_q(first + 1, 1, 1)
                turn_q(first, 0, 0)
                turn_q(first, 0, 1)
                pe.wait_ge(S["ctx_ready"], HC * (b + 1))
                product_y(first, 0)
                product_y(first, 1)
                product_q(first + 2, 2, 0)
                product_q(first + 2, 2, 1)
                turn_q(first + 1, 1, 0)
                turn_q(first + 1, 1, 1)
                product_y(first + 1, 0)
                product_y(first + 1, 1)
                if b == 0:
                    pe.wait_ge(S["wo_ready"], 1)

                def step_c(i, g, a, more_q=True, more_y=True):
                    turn_s(g, a, 0)
                    if more_q:
                        product_q(g + 3, i + 3, 0)
                    product_out(g, 0)
                    if more_y:
                        turn_q(g + 2, a, 0)
                        turn_q(g + 2, a, 1)
                    turn_s(g, a, 1)
                    if more_q:
                        product_q(g + 3, i + 3, 1)
                    if more_y:
                        product_y(g + 2, 0)
                    product_out(g, 1)
                    if more_y:
                        product_y(g + 2, 1)

                step_c(0, first, 0)
                with pe.Fori(0, (NP - 4) // 2) as n:
                    step_c(n * 2 + 1, n * 2 + (first + 1), 1)
                    step_c(n * 2 + 2, n * 2 + (first + 2), 0)
                step_c(NP - 3, first + NP - 3, (NP - 3) % 2, False, True)
                step_c(NP - 2, first + NP - 2, (NP - 2) % 2, False, False)
                if b + 1 < B:
                    pe.wait_ge(S["q_evac"], first + NP)
                    turn_z(first + NP, 0)
                step_c(NP - 1, first + NP - 1, (NP - 1) % 2, False, False)



_INS = ["x", "cond_1024"] + ["L0_cond_" + n for n in (
    "norm_g", "norm_b", "Wq", "bq", "Wk", "bk", "Wv", "bv", "emb_W", "emb_b", "sn_g", "sn_b", "out_W", "out_b")]


def kernel(**inputs):
    import numpy as np
    from concourse import bacc
    from concourse.bass_utils import run_bass_kernel_spmd

    nc = bacc.Bacc("TRN2", target_bir_lowering=False, num_devices=1)
    arrays, args = {}, []
    for name in _INS:
        a = np.ascontiguousarray(inputs[name])
        arrays[f"in_{name}_dram"] = a
        args.append(nc.dram_tensor(f"in_{name}_dram", a.shape, mybir.dt.from_np(a.dtype), kind="ExternalInput").ap())
    shape = arrays["in_x_dram"].shape
    args.append(nc.dram_tensor("out_0_dram", shape, F32, kind="ExternalOutput").ap())
    linear_attention_block(nc, *args)
    r = run_bass_kernel_spmd(nc, [arrays], core_ids=[0])
    return r.results[0]["out_0_dram"]
```

```python
import math
from contextlib import ExitStack

import concourse.bass as bass
from concourse import mybir

F32 = mybir.dt.float32
F16 = mybir.dt.float16
I32 = mybir.dt.int32
ALU = mybir.AluOpType
ACT = mybir.ActivationFunctionType
AX = mybir.AxisListType

P = 128
HEADS = 16
EPS = 1e-5
Z_SCALE = 256.0
EK_SHIFT = 15 * math.log(2.0)
TOP = 8192.0
EXPONENT = 0x7F800000
GUESS = 0x5F3759DF - (1 << 22) - (1 << 31)
X_STEPS = 16
Y_STEPS = 9
LOWEST = -3.4028234e38


def linear_attention_block(nc, x, cond, norm_g, norm_b, Wq, bq, Wk, bk, Wv, bv, emb_W, emb_b,
                           sn_g, sn_b, out_W, out_b, out):
    B, T, D = x.shape
    C = D // P
    DH = D // HEADS
    HC = P // DH
    NP = T // (2 * P)
    YW = HC * (DH + 1)
    NR = (2 + B) * C

    x_v = x.rearrange("b (i p u) c -> (b i) p u c", p=P, u=2)
    out_v = out.rearrange("b (i p u) c -> (b i) p u c", p=P, u=2)

    def chunked(w):
        return w.rearrange("(j p) n -> p j n", p=P)

    def rows(v):
        return v.rearrange("(j p) -> j p", p=P)

    with ExitStack() as ctx:
        def sb(name, shape, dt=F32):
            return ctx.enter_context(nc.sbuf_tensor(name, shape, dt))

        def sem(name):
            return ctx.enter_context(nc.semaphore(name))

        wk = sb("wk", [P, 2, C, D], F16)
        wq = sb("wq", [P, 2, C, D], F16)
        wo = sb("wo", [P, 2, C, D], F16)
        wv = sb("wv", [P, C, D])
        NB = 3 + 4 * B
        wide = sb("wide", [P, NB, D])
        kb_row, qb_row, vb_row = wide[:, 0, :], wide[:, 1, :], wide[:, 2, :]

        def batch_row(kind, b):
            return wide[:, 3 + 4 * b + kind, :]
        MUL, ADD, GOB, GATE = range(4)

        ident = sb("ident", [P, P])
        ident16 = sb("ident16", [P, P], F16)
        ones = sb("ones", [P, P])
        z256 = sb("z256", [P, 1])
        cols = sb("cols", [P, NR])
        prm = sb("prm", [NR, P])
        silu2 = sb("silu2", [P, B * C])
        silu_t = sb("silu_t", [P, B * C])
        size_c = sb("size_c", [P, C])
        stat = sb("stat", [P, 3])
        stat_m = sb("stat_m", [1, 1])
        norm_top = sb("norm_top", [P, 2, C])
        pow2 = sb("pow2", [P, 3 + B])
        top_r = sb("top_r", [P, 3 + B])
        bound = sb("bound", [B, 2])
        bound_d = sb("bound_d", [B, B])
        inv_k, inv_q = sb("inv_k", [P, 1]), sb("inv_q", [P, 1])
        inv_o = sb("inv_o", [P, B])

        zh = sb("zh", [P, 2 * NP, D], F16)
        zl = sb("zl", [P, 2 * NP, D], F16)
        zT = sb("zT", [P, 2 * NP, 2, C, P], F16)
        k_all = sb("k_all", [P, NP, 2, D])
        x_in = sb("x_in", [P, 4, 2, D])
        z_sb = sb("z_sb", [P, 2, 2, D])
        bn6 = sb("bn6", [P, 2, 6])
        mv = sb("mv", [P, 2, 2])
        half_v = sb("half_v", [P, 2])
        root = sb("root", [P, 2, 2])
        root_t = sb("root_t", [P, 2])
        z_nmr = sb("z_nmr", [P, 2, 2])
        acc = sb("acc", [P, 2, D])
        m_col = sb("m_col", [P, C])
        m_diag = sb("m_diag", [P, C, P])
        m_row = m_diag[:, :, :].rearrange("p j c -> p (j c)")
        ek = sb("ek", [P, 2, 2, D])
        ekh, ekl = (x_in[:, n, :, :].rearrange("p u c -> p (u c)").bitcast(F16)
                    .rearrange("p (a u c) -> p a u c", a=2, u=2) for n in (2, 3))
        r_s = sb("r_s", [P, C])
        ctx_bd = sb("ctx_bd", [P, C, HC, DH + 1])
        q_sb = sb("q_sb", [P, 2, 2, D])
        q_max = sb("q_max", [P, 2, 2, HEADS])
        eqT = sb("eqT", [P, 2, C, P])
        r_q = sb("r_q", [P, 2, HEADS])
        y_bn6 = sb("y_bn6", [P, 2, 6])
        y_mv = sb("y_mv", [P, 2, 2])
        y_half_v = sb("y_half_v", [P, 2])
        y_root = sb("y_root", [P, 2, 2])
        y_root_t = sb("y_root_t", [P, 2])
        spot = sb("spot", [P, 2, 1])
        y_nmr = sb("y_nmr", [P, 2, 2])

        gT = ek[:, :, :, :].rearrange("p a u c -> p (a u) c")
        y_sb = ek
        spare = k_all[:, :, :, :].rearrange("p i u c -> p (i u c)")
        PAIR = 2 * D
        t_sb = spare[:, 0:PAIR].rearrange("p (u c) -> p u c", u=2)
        sT = spare[:, PAIR:2 * PAIR].bitcast(F16).rearrange("p (s u j c) -> p s u j c", s=2, u=2, j=C)
        fo = spare[:, 2 * PAIR:4 * PAIR].rearrange("p (a u c) -> p a u c", a=2, u=2)
        xr = spare[:, 4 * PAIR:8 * PAIR].rearrange("p (a u c) -> p a u c", a=4, u=2)
        wk_raw, wo_raw = (spare[:, n * C * D:(n + 1) * C * D].rearrange("p (j n) -> p j n", j=C) for n in range(2))
        wq_raw = wk_raw
        SNG, SNB, OUTB, COND, EMBB, EMB = 3, 4, 5, 6, 7, 9
        emb_a = ek[:, :, :, :].rearrange("p a u c -> p (a u) c").rearrange("p (j h) c -> p j (h c)", h=2)
        emb_b2 = q_sb[:, :, :, :].rearrange("p a u c -> p (a u) c").rearrange("p (j h) c -> p j (h c)", h=2)

        scratch = nc.dram_tensor("rows_scratch", [B, 4 * D], F32, kind="Internal").ap()

        ps = ctx.enter_context(nc.psum_tensor("ps", [P, 8, D], F32))
        ps16 = ps[:, :, :].bitcast(F16)
        Q_BANK, K_BANK, EQT_BANK, Y_BANK, OUT_BANK, ST_BANK = 0, 2, 2, 4, 6, 7
        G_BANK, M_BANK, CTX_BANK = 2, 6, 6

        names = """prm_in bias_in rows_in x_in_done wk_in wq_in wv_in wo_in emb_in const_ready prm_T cols_ready
            silu_ready silu2_ready emb_done emb_kept scr_out wide_in stat_ready statT stat_max_done
            stat_b bias_done bias_ready wk_hi w_scaled w_high wk_ready w_ready wv_ready row_step bound_diag bound_b
            scales_ready setup_step x_stats x_step stat_ready_z z_ready zh_ready zl_ready t_done zT_ready
            k_done k_ready kmax_done kT_done mdiag_ready mrow_done mrow_ready acc_cleared
            ksub_done exp_done ekh_ready ekl_ready s_done g_pair s_sum gT_ready ctx_done ctx_step ctx_ready
            q_done q_evac qmax_done qsub_done qexp_done eqT_done eqT_ready y_done y_ready y_stats y_step
            ystat_ready gated n_ready mul_ready h_ready tanh_ready s_ready sT_done sh_ready sl_ready o_done
            fin_ready xr_in xg_ready out_ready stored rq_step""".split()
        S = {n: sem(n) for n in names}

        block = ctx.enter_context(nc.Block())

        def starts(g, n):
            return isinstance(g, int) and g < n

        def ahead(i, g, u, n):
            return i + (u + n) // 2, g + (u + n) // 2, (u + n) % 2

        def lives(i):
            return not isinstance(i, int) or 0 <= i < NP

        def over_tiles(eng, b, peel, step):
            first = b * NP
            for u in range(-1, 2 * peel):
                step(u // 2, first + u // 2, u % 2)
            with eng.Fori(peel, NP - 3) as i:
                for u in range(2):
                    step(i, i + first, u)

        def over_pairs(eng, b, peel, end, step):
            first = b * NP
            peeled = peel if b == 0 else 0
            for i in range(peeled):
                step(i, first + i)
            with eng.Fori(peeled, end) as i:
                step(i, i + first)

        @block.sync
        def _(sp):
            sp.dma_start(x_in[:, 0, :, :], x_v[0]).then_inc(S["x_in_done"], 16)
            sp.dma_start(wk_raw, chunked(Wk)).then_inc(S["wk_in"], 16)
            for n in range(1, 4):
                sp.wait_ge(S["x_in_done"], 16 * n)
                sp.dma_start(x_in[:, n, :, :], x_v[n]).then_inc(S["x_in_done"], 16)
            sp.dma_start(emb_a, chunked(emb_W)[:, 0:2, :]).then_inc(S["emb_in"], 16)
            sp.dma_start(emb_b2, chunked(emb_W)[:, 2:4, :]).then_inc(S["emb_in"], 16)
            sp.dma_start(wv[:, :, :], chunked(Wv)).then_inc(S["wv_in"], 16)

            def load_x(g):
                sp.wait_ge(S["x_in_done"], 16 * g)
                if not starts(g, 4):
                    sp.wait_ge(S["z_ready"], 2 * g - 6)
                sp.dma_start(x_in[:, g % 4, :, :], x_v[g]).then_inc(S["x_in_done"], 16)

            def load_residual(g):
                if not starts(g, 1):
                    sp.wait_ge(S["xr_in"], 16 * g)
                sp.dma_start(xr[:, g % 4, :, :], x_v[g]).then_inc(S["xr_in"], 16)

            def store(g):
                if not starts(g, 1):
                    sp.wait_ge(S["stored"], 16 * g)
                sp.wait_ge(S["out_ready"], 2 * g + 2)
                sp.dma_start(out_v[g], fo[:, g % 2, :, :]).then_inc(S["stored"], 16)

            for b in range(B):
                first = b * NP
                for i in range(4 if b == 0 else 6, NP):
                    load_x(first + i)
                if b + 1 < B:
                    load_x(first + NP)
                    load_x(first + NP + 1)
                if b == 0:
                    sp.wait_ge(S["ksub_done"], 2)
                    sp.dma_start(wq_raw, chunked(Wq)).then_inc(S["wq_in"], 16)
                    sp.wait_ge(S["ksub_done"], 4)
                    sp.dma_start(wo_raw, chunked(out_W)).then_inc(S["wo_in"], 16)
                    sp.wait_ge(S["bound_diag"], 1)
                    sp.dma_start(scratch.rearrange("b (r n) -> b r n", n=D), wide[0:B, 3:7, :]).then_inc(S["scr_out"], 16)
                    sp.wait_ge(S["scr_out"], 16)
                    sp.dma_start(wide[:, 3:NB, :].rearrange("p n c -> p (n c)"),
                                 scratch.rearrange("b r -> (b r)").rearrange("(o r) -> o r", o=1)
                                 .broadcast_to([P, 4 * B * D])).then_inc(S["wide_in"], 16)
                sp.wait_ge(S["ksub_done"], first + NP)
                for i in range(4):
                    load_residual(first + i)
                def step(i, g):
                    store(g)
                    load_residual(g + 4)

                if b + 1 < B:
                    sp.wait_ge(S["g_pair"], first + NP)
                    load_x(first + NP + 2)
                    load_x(first + NP + 3)
                    load_x(first + NP + 4)
                    load_x(first + NP + 5)
                over_pairs(sp, b, 1, NP - 4, step)
                for i in range(NP - 4, NP):
                    store(first + i)
            sp.wait_ge(S["stored"], 16 * B * NP)

        @block.gpsimd
        def _(pool):
            pool.memset(ident[:, :], 0.0).then_inc(S["const_ready"], 1)
            pool.memset(ones[:, :], 1.0).then_inc(S["const_ready"], 1)
            pool.wait_ge(S["const_ready"], 2)
            pool.affine_select(out=ident[:, :], in_=ident[:, :], compare_op=ALU.not_equal, fill=1.0, base=0,
                               pattern=[[-1, P]], channel_multiplier=1).then_inc(S["const_ready"], 1)
            pool.wait_ge(S["const_ready"], 3)
            pool.tensor_copy(ident16[:, :], ident[:, :]).then_inc(S["const_ready"], 1)

            def low_z(g, i):
                pool.wait_ge(S["zh_ready"], g + 1)
                pool.tensor_tensor(zl[:, bass.ts(i, 2), :], z_sb[:, g % 2, :, :], zh[:, bass.ts(i, 2), :],
                                   ALU.subtract).then_inc(S["zl_ready"], 1)

            def modulation_rows():
                def row(n):
                    return wide[0:B, n, :]

                def link(n, out_row, a, c, op):
                    pool.tensor_tensor(out_row, a, c, op).then_inc(S["row_step"], 1)
                    pool.wait_ge(S["row_step"], n)

                pool.wait_ge(S["rows_in"], 80)
                pool.wait_ge(S["emb_kept"], 1)
                link(1, wide[0:B, EMB:EMB + 2, :], wide[0:B, EMB:EMB + 2, :], wide[0:B, EMBB:EMBB + 2, :], ALU.add)
                link(2, row(EMB), row(EMB), ones[0:B, 0:1].broadcast_to([B, D]), ALU.add)
                link(3, row(SNG), row(SNG), row(EMB), ALU.mult)
                link(4, row(SNB), row(SNB), row(EMB), ALU.mult)
                link(5, row(SNB), row(SNB), row(EMB + 1), ALU.add)
                link(6, row(OUTB), row(OUTB), row(COND), ALU.mult)

            def sub_max(g, i):
                if not starts(g, 2):
                    pool.wait_ge(S["s_done"], g - 1)
                    pool.wait_ge(S["ekl_ready"], g - 1)
                pool.tensor_tensor(ek[:, g % 2, :, :], k_all[:, i, :, :],
                                   m_row.rearrange("p (o c) -> p o c", o=1).broadcast_to([P, 2, D]),
                                   ALU.subtract).then_inc(S["ksub_done"], 1)

            def split_low(w, raw, n):
                pool.wait_ge(S["w_high"], n)
                pool.tensor_tensor(w[:, 1, :, :], raw, w[:, 0, :, :], ALU.subtract).then_inc(S["w_ready"], 1)

            def sub_q_max(g, u):
                pool.wait_ge(S["qmax_done"], 2 * g + u + 1)
                q = q_sb[:, g % 2, u, :].rearrange("p (h d) -> p h d", d=DH)
                m = q_max[:, g % 2, u, :].rearrange("p (h o) -> p h o", o=1)
                pool.tensor_tensor(q, q, m.broadcast_to([P, HEADS, DH]), ALU.subtract).then_inc(S["qsub_done"], 1)

            def modulate(g, u, b):
                pool.wait_ge(S["n_ready"], 2 * g + u + 1)
                y = y_sb[:, g % 2, u, :]
                pool.tensor_tensor(y, y, batch_row(MUL, b), ALU.mult).then_inc(S["mul_ready"], 1)

            def residual(g, u, b):
                pool.wait_ge(S["xr_in"], 16 * g + 16)
                r = xr[:, g % 4, u, :]
                pool.tensor_tensor(r, r, batch_row(GOB, b), ALU.add).then_inc(S["xg_ready"], 1)

            def add_residual(g, u, b):
                pool.wait_ge(S["fin_ready"], 2 * g + u + 1)
                pool.tensor_tensor(fo[:, g % 2, u, :], fo[:, g % 2, u, :], batch_row(GATE, b),
                                   ALU.mult).then_inc(S["gated"], 1)
                pool.wait_ge(S["wide_in"], 16)
                pool.wait_ge(S["gated"], 2 * g + u + 1)
                pool.wait_ge(S["xg_ready"], 2 * g + u + 1)
                pool.tensor_tensor(fo[:, g % 2, u, :], fo[:, g % 2, u, :], xr[:, g % 4, u, :],
                                   ALU.add).then_inc(S["out_ready"], 1)

            for b in range(B):
                first = b * NP
                if b == 0:
                    for n in range(3):
                        low_z(n, n)
                if b > 0:
                    pool.wait_ge(S["s_sum"], b)
                pool.memset(acc[:, :, :], LOWEST).then_inc(S["acc_cleared"], 1)
                with pool.Fori(3, NP) as i:
                    low_z(i + first, i)
                pool.wait_ge(S["kT_done"], b + 1)
                pool.memset(acc[:, :, :], 0.0).then_inc(S["acc_cleared"], 1)
                pool.wait_ge(S["mrow_ready"], b + 1)
                if b > 0:
                    pool.wait_ge(S["ctx_done"], b)
                if b == 0:
                    pool.wait_ge(S["emb_done"], 1)
                sub_max(first, 0)
                sub_max(first + 1, 1)
                if b + 1 < B:
                    for i in range(2, NP):
                        sub_max(first + i, i)
                        if i == 3:
                            modulation_rows()
                        if i in (5, 7):
                            low_z(first + NP + i // 2 - 2, i // 2 - 2)
                        if i == 6:
                            split_low(wq, wq_raw, 1)
                if b == 0:
                    split_low(wo, wo_raw, 2)
                else:
                    with pool.Fori(2, NP) as i:
                        sub_max(i + first, i)
                for u in range(4):
                    sub_q_max(first + u // 2, u % 2)
                if b == 0:
                    pool.wait_ge(S["wide_in"], 16)

                def step(i, g, u):
                    i1, g1, u1 = ahead(i, g, u, 1)
                    i4, g4, u4 = ahead(i, g, u, 4)
                    i0, g0, u0 = ahead(i, g, u, -2)
                    if lives(i4) and not (isinstance(i4, int) and i4 < 2):
                        sub_q_max(g4, u4)
                    if lives(i1):
                        modulate(g1, u1, b)
                    if lives(i):
                        residual(g, u, b)
                    if lives(i0):
                        add_residual(g0, u0, b)

                over_tiles(pool, b, 1, step)
                for i in range(NP - 3, NP + 1):
                    step(i, first + i, 0)
                    step(i, first + i, 1)
                if b + 1 < B:
                    low_z(first + NP + 2, 2)

        @block.scalar
        def _(act):
            for n, v in enumerate((norm_g, norm_b)):
                act.dma_start(prm[n * C:(n + 1) * C, :], rows(v)).then_inc(S["prm_in"], 16)
            act.dma_start(prm[2 * C:NR, :], cond.rearrange("b (j p) -> (b j) p", p=P)).then_inc(S["prm_in"], 16)
            for n, v in enumerate((bk, bq, bv)):
                act.dma_start(wide[0:1, n, :], v.rearrange("(o c) -> o c", o=1)).then_inc(S["bias_in"], 16)
            for n, v in ((SNG, sn_g), (SNB, sn_b), (OUTB, out_b)):
                act.dma_start(wide[0:B, n, :], v.rearrange("(o c) -> o c", o=1).broadcast_to([B, D])
                              ).then_inc(S["rows_in"], 16)
            act.dma_start(wide[0:B, EMBB:EMBB + 2, :].rearrange("b n c -> b (n c)"),
                          emb_b.rearrange("(o c) -> o c", o=1).broadcast_to([B, 2 * D])).then_inc(S["rows_in"], 16)
            act.dma_start(wide[0:B, COND, :], cond).then_inc(S["rows_in"], 16)
            act.wait_ge(S["cols_ready"], 1)
            act.activation(silu_t[:, :], cols[:, 2 * C:NR], ACT.Tanh, scale=0.5).then_inc(S["silu_ready"], 1)

            def keep_out(g, u, b):
                act.wait_ge(S["o_done"], 2 * g + u + 1)
                if u == 0 and not starts(g, 2):
                    act.wait_ge(S["stored"], 16 * g - 16)
                act.activation(fo[:, g % 2, u, :], ps[:, OUT_BANK, :], ACT.Identity,
                               scale=inv_o[:, b:b + 1]).then_inc(S["fin_ready"], 1)

            def normalise_z(g):
                act.wait_ge(S["stat_ready_z"], g + 1)
                if not starts(g, 2):
                    act.wait_ge(S["zl_ready"], g - 1)
                for u in range(2):
                    act.activation(z_sb[:, g % 2, u, :], x_in[:, g % 4, u, :], ACT.Identity,
                                   bias=z_nmr[:, g % 2, u:u + 1],
                                   scale=root[:, g % 2, u:u + 1]).then_inc(S["z_ready"], 1)

            def high_z(g, i):
                act.wait_ge(S["z_ready"], 2 * g + 2)
                act.activation(zh[:, bass.ts(i, 2), :], z_sb[:, g % 2, :, :], ACT.Copy).then_inc(S["zh_ready"], 1)

            def keep_zT(g, i, u):
                if u == 0:
                    act.wait_ge(S["t_done"], 2 * g + 2)
                act.activation(zT[:, 2 * i + u, :, :, :].rearrange("p s j c -> p (s j c)"), ps16[:, Q_BANK + u, :],
                               ACT.Copy).then_inc(S["zT_ready"], 1)

            def exp_k(g):
                act.wait_ge(S["ksub_done"], g + 1)
                e = ek[:, g % 2, :, :]
                act.activation(e, e, ACT.Exp).then_inc(S["exp_done"], 1)
                act.wait_ge(S["exp_done"], g + 1)
                if not starts(g, 2):
                    act.wait_ge(S["g_pair"], g - 1)
                act.activation(ekh[:, g % 2, :, :], e, ACT.Copy).then_inc(S["ekh_ready"], 1)

            def exp_q(g, u):
                act.wait_ge(S["qsub_done"], 2 * g + u + 1)
                q = q_sb[:, g % 2, u, :]
                act.activation(q, q, ACT.Exp).then_inc(S["qexp_done"], 1)

            def keep_eqT(g, u):
                act.wait_ge(S["eqT_done"], 2 * g + u + 1)
                if not starts(g, 1):
                    act.wait_ge(S["y_done"], 2 * g + u - 1)
                act.activation(eqT[:, u, :, :].rearrange("p j c -> p (j c)"), ps[:, EQT_BANK + u, :],
                               ACT.Copy).then_inc(S["eqT_ready"], 1)

            def normalise_y(g, u):
                act.wait_ge(S["ystat_ready"], 2 * g + u + 1)
                y = y_sb[:, g % 2, u, :]
                act.activation(y, y, ACT.Identity, bias=y_nmr[:, g % 2, u:u + 1],
                               scale=y_root[:, g % 2, u:u + 1]).then_inc(S["n_ready"], 1)

            def tanh_h(g, u):
                act.wait_ge(S["cols_ready"], 1)
                act.wait_ge(S["h_ready"], 2 * g + u + 1)
                act.activation(t_sb[:, u, :], y_sb[:, g % 2, u, :], ACT.Tanh, scale=0.5).then_inc(S["tanh_ready"], 1)

            def high_s(g, u, b):
                act.wait_ge(S["sT_done"], 2 * g + u + 1)
                if not starts(g, 1):
                    act.wait_ge(S["o_done"], 2 * g + u - 1)
                act.activation(sT[:, 0, u, :, :].rearrange("p j c -> p (j c)"), ps[:, ST_BANK, :], ACT.Identity,
                               scale=top_r[:, 3 + b:4 + b]).then_inc(S["sh_ready"], 1)

            def keep_row(n, bank):
                act.wait_ge(S["bias_done"], n + 1)
                act.activation(wide[:, n, :], ps[:, bank, :], ACT.Copy).then_inc(S["bias_ready"], 1)

            def scale_split_high(w, raw, n):
                act.wait_ge(S["scales_ready"], n + 1)
                if n == 1:
                    act.wait_ge(S["bias_done"], 3)
                    for j in range(C):
                        act.activation(raw[:, j, :], raw[:, j, :], ACT.Identity,
                                       scale=norm_top[:, 1, j:j + 1]).then_inc(S["w_scaled"], 1)
                else:
                    act.activation(raw, raw, ACT.Identity, scale=top_r[:, 2:3]).then_inc(S["w_scaled"], 1)
                act.wait_ge(S["w_scaled"], C * min(n, 1) + (n - 1))
                act.activation(w[:, 0, :, :], raw, ACT.Copy).then_inc(S["w_high"], 1)

            normalise_z(0)
            high_z(0, 0)
            act.wait_ge(S["scales_ready"], 1)
            for j in range(C):
                act.activation(wk[:, 0, j, :], wk_raw[:, j, :], ACT.Identity,
                               scale=norm_top[:, 0, j:j + 1]).then_inc(S["wk_hi"], 1)
            keep_row(0, 6)
            keep_zT(0, 0, 0)
            keep_zT(0, 0, 1)
            for n in range(1, 3):
                normalise_z(n)
                high_z(n, n)
            for b in range(B):
                first = b * NP
                def step_a(i, g):
                    for u in range(2):
                        keep_zT(g + 1, i + 1, u)
                    normalise_z(g + 3)
                    high_z(g + 3, i + 3)

                over_pairs(act, b, 1, NP - 3, step_a)
                for i in range(NP - 2, NP):
                    for u in range(2):
                        keep_zT(first + i, i, u)
                if b == 0:
                    act.wait_ge(S["emb_done"], 1)
                    act.activation(wide[0:B, EMB:EMB + 2, :], ps[0:B, K_BANK:K_BANK + 2, :], ACT.Copy,
                                   scale=0.5).then_inc(S["emb_kept"], 1)
                    act.wait_ge(S["bias_done"], 2)
                    act.activation(wide[:, 2, :], ps[:, K_BANK + 2, :], ACT.Copy).then_inc(S["bias_ready"], 1)
                    for j in range(C):
                        act.activation(wv[:, j, :], wv[:, j, :], ACT.Identity,
                                       scale=cols[:, j:j + 1]).then_inc(S["wv_ready"], 1)
                exp_k(first)
                exp_k(first + 1)
                if b + 1 < B:
                    for i in range(2, NP):
                        exp_k(first + i)
                        if i == 5:
                            scale_split_high(wq, wq_raw, 1)
                        if i in (4, 6):
                            n = i // 2 - 2
                            normalise_z(first + NP + n)
                            act.wait_ge(S["g_pair"], first + n + 1)
                            high_z(first + NP + n, n)
                else:
                    with act.Fori(2, NP) as i:
                        exp_k(i + first)
                if b == 0:
                    act.wait_ge(S["bias_done"], 3)
                    act.activation(wide[:, 1, :], ps[:, 6, :], ACT.Copy).then_inc(S["bias_ready"], 1)
                    scale_split_high(wo, wo_raw, 2)
                act.wait_ge(S["g_pair"], first + NP)
                act.wait_ge(S["s_done"], first + NP)
                act.activation(gT[:, 0:2, :], ps[:, G_BANK:G_BANK + 2, :], ACT.Copy).then_inc(S["gT_ready"], 1)
                for t in range(3):
                    exp_q(first + t // 2, t % 2)

                def step(i, g, u):
                    i0, g0, u0 = ahead(i, g, u, -1)
                    i9, g9, u9 = ahead(i, g, u, -2)
                    i1, g1, u1 = ahead(i, g, u, 1)
                    i3, g3, u3 = ahead(i, g, u, 3)
                    i4, g4, u4 = ahead(i, g, u, 4)
                    if lives(i0):
                        high_s(g0, u0, b)
                    if lives(i1):
                        normalise_y(g1, u1)
                    if lives(i3):
                        keep_eqT(g3, u3)
                    if lives(i9):
                        keep_out(g9, u9, b)
                    if lives(i4) and not (isinstance(i4, int) and i4 < 2):
                        exp_q(g4, u4)
                    if lives(i1):
                        tanh_h(g1, u1)

                step(-2, first - 2, 1)
                step(-1, first - 1, 0)
                exp_q(first + 1, 1)
                over_tiles(act, b, 3, step)
                for i in range(NP - 3, NP + 1):
                    step(i, first + i, 0)
                    if i == NP - 1 and b + 1 < B:
                        keep_zT(first + NP, 0, 0)
                        keep_zT(first + NP, 0, 1)
                    step(i, first + i, 1)
                if b + 1 < B:
                    normalise_z(first + NP + 2)
                    high_z(first + NP + 2, 2)

        @block.vector
        def _(dve):
            def newton_square(y, half, tmp):
                return dve.scalar_tensor_tensor(out=tmp, in0=y, scalar=y, in1=half, op0=ALU.mult, op1=ALU.mult)

            def newton_root(y, tmp):
                return dve.scalar_tensor_tensor(out=y, in0=tmp, scalar=-1.5, in1=y, op0=ALU.add, op1=ALU.mult)

            def first_guess(y, half):
                return dve.tensor_scalar(y.bitcast(I32), half.bitcast(I32), -0.5, float(GUESS), ALU.mult, ALU.add)

            def stats_x(g, u):
                dve.wait_ge(S["x_in_done"], 16 * g + 16)
                if not starts(g, 1):
                    dve.wait_ge(S["x_step"], X_STEPS * g - X_STEPS + 2)
                dve.bn_stats(bn6[:, u, :], x_in[:, g % 4, u, :]).then_inc(S["x_stats"], 1)

            def aggregate_x(g):
                if not starts(g, 1):
                    dve.wait_ge(S["stat_ready_z"], g)
                dve.wait_ge(S["x_stats"], 2 * g + 2)
                dve.memset(root_t[:, :], 0.0)
                for u in range(2):
                    dve.bn_aggr(mv[:, u, :], bn6[:, u, :]).then_inc(S["x_step"], 1)

            def halve_x(g):
                dve.wait_ge(S["x_step"], X_STEPS * g + 2)
                dve.tensor_scalar(half_v[:, :], mv[:, :, 1], EPS, 0.5 / Z_SCALE ** 2, ALU.add,
                                  ALU.mult).then_inc(S["x_step"], 1)

            def guess_x(g):
                if not starts(g, 2):
                    dve.wait_ge(S["z_ready"], 2 * g - 2)
                dve.wait_ge(S["x_step"], X_STEPS * g + 3)
                first_guess(root[:, g % 2, :], half_v[:, :]).then_inc(S["x_step"], 1)

            def square_x(g, n):
                dve.wait_ge(S["x_step"], X_STEPS * g + 4 * n + 4)
                for u in range(2):
                    newton_square(root[:, g % 2, u:u + 1], half_v[:, u:u + 1],
                                  root_t[:, u:u + 1]).then_inc(S["x_step"], 1)

            def root_x(g, n):
                dve.wait_ge(S["x_step"], X_STEPS * g + 4 * n + 6)
                for u in range(2):
                    newton_root(root[:, g % 2, u:u + 1], root_t[:, u:u + 1]).then_inc(S["x_step"], 1)

            def finish_x(g):
                dve.wait_ge(S["x_step"], X_STEPS * g + 16)
                dve.scalar_tensor_tensor(out=z_nmr[:, g % 2, :], in0=mv[:, :, 0], scalar=-1.0,
                                         in1=root[:, g % 2, :], op0=ALU.mult,
                                         op1=ALU.mult).then_inc(S["stat_ready_z"], 1)

            def front(g):
                for u in range(2):
                    stats_x(g, u)
                aggregate_x(g)
                halve_x(g)
                guess_x(g)
                for n in range(3):
                    square_x(g, n)
                    root_x(g, n)
                finish_x(g)

            def keep_k(g, i, u):
                bank = K_BANK + 2 * (g % 2) + u
                dve.wait_ge(S["k_done"], 2 * g + u + 1)
                dve.scalar_tensor_tensor(out=k_all[:, i, u, :], in0=ps[:, bank, :], scalar=inv_k[:, 0:1],
                                         in1=kb_row, op0=ALU.mult, op1=ALU.add).then_inc(S["k_ready"], 1)

            def running_max(g, i, u):
                dve.wait_ge(S["k_ready"], 2 * g + u + 1)
                if not starts(g, 1):
                    dve.wait_ge(S["kmax_done"], 2 * g + u - 1)
                dve.tensor_tensor(acc[:, u, :], acc[:, u, :], k_all[:, i, u, :], ALU.max).then_inc(S["kmax_done"], 1)

            def split_ek(g):
                dve.wait_ge(S["ekh_ready"], g + 1)
                if not starts(g, 2):
                    dve.wait_ge(S["g_pair"], g - 1)
                dve.tensor_tensor(ekl[:, g % 2, :, :], ek[:, g % 2, :, :], ekh[:, g % 2, :, :],
                                  ALU.subtract).then_inc(S["ekl_ready"], 1)
                if not starts(g, 1):
                    dve.wait_ge(S["s_done"], g)
                dve.tensor_tensor(acc[:, :, :], acc[:, :, :], ek[:, g % 2, :, :], ALU.add).then_inc(S["s_done"], 1)

            def keep_q(g, u):
                dve.wait_ge(S["q_done"], 2 * g + u + 1)
                if not starts(g, 2):
                    dve.wait_ge(S["eqT_done"], 2 * g + u - 3)
                dve.scalar_tensor_tensor(out=q_sb[:, g % 2, u, :], in0=ps[:, Q_BANK + u, :], scalar=inv_q[:, 0:1],
                                         in1=qb_row, op0=ALU.mult, op1=ALU.add).then_inc(S["q_evac"], 1)

            def max_q(g, u):
                dve.wait_ge(S["q_evac"], 2 * g + u + 1)
                dve.tensor_reduce(q_max[:, g % 2, u, :], q_sb[:, g % 2, u, :].rearrange("p (h d) -> p h d", d=DH),
                                  AX.X, ALU.max).then_inc(S["qmax_done"], 1)

            both = ps[:, Y_BANK:Y_BANK + 2, 0:2 * YW].rearrange("p a (h d) -> p a h d", d=DH + 1)

            def invert_sum(g, u):
                dve.wait_ge(S["y_done"], 2 * g + u + 1)
                dve.reciprocal(r_q[:, u, :].rearrange("p (a h o) -> p a h o", a=2, o=1),
                               both[:, :, :, DH:DH + 1]).then_inc(S["rq_step"], 1)

            def keep_y(g, u):
                dve.wait_ge(S["rq_step"], 2 * g + u + 1)
                if not starts(g, 2):
                    dve.wait_ge(S["sT_done"], 2 * g + u - 3)
                dve.tensor_tensor(y_sb[:, g % 2, u, :].rearrange("p (a h d) -> p a h d", a=2, d=DH),
                                  both[:, :, :, 0:DH],
                                  r_q[:, u, :].rearrange("p (a h o) -> p a h o", a=2, o=1)
                                  .broadcast_to([P, 2, HEADS // 2, DH]), ALU.mult).then_inc(S["y_ready"], 1)

            def stats_y(g, u):
                dve.wait_ge(S["y_ready"], 2 * g + u + 1)
                dve.memset(spot[:, u, 0:1], 0.0)
                dve.bn_stats(y_bn6[:, u, :], y_sb[:, g % 2, u, :]).then_inc(S["y_stats"], 1)

            def y_at(g, u):
                return g * (2 * Y_STEPS) + u * Y_STEPS

            def aggregate_y(g, u):
                dve.wait_ge(S["y_stats"], 2 * g + u + 1)
                dve.memset(y_root_t[:, u:u + 1], 0.0)
                dve.bn_aggr(y_mv[:, u, :], y_bn6[:, u, :]).then_inc(S["y_step"], 1)

            def halve_y(g, u):
                dve.wait_ge(S["y_step"], y_at(g, u) + 1)
                dve.tensor_scalar(y_half_v[:, u:u + 1], y_mv[:, u, 1:2], EPS, 0.5, ALU.add,
                                  ALU.mult).then_inc(S["y_step"], 1)

            def guess_y(g, u):
                dve.wait_ge(S["y_step"], y_at(g, u) + 2)
                first_guess(y_root[:, g % 2, u:u + 1], y_half_v[:, u:u + 1]).then_inc(S["y_step"], 1)

            def square_y(g, u, n):
                dve.wait_ge(S["y_step"], y_at(g, u) + 2 * n + 3)
                newton_square(y_root[:, g % 2, u:u + 1], y_half_v[:, u:u + 1],
                              y_root_t[:, u:u + 1]).then_inc(S["y_step"], 1)

            def root_y(g, u, n):
                dve.wait_ge(S["y_step"], y_at(g, u) + 2 * n + 4)
                newton_root(y_root[:, g % 2, u:u + 1], y_root_t[:, u:u + 1]).then_inc(S["y_step"], 1)

            def finish_y(g, u):
                dve.wait_ge(S["y_step"], y_at(g, u) + 9)
                dve.scalar_tensor_tensor(out=y_nmr[:, g % 2, u:u + 1], in0=y_mv[:, u, 0:1], scalar=-1.0,
                                         in1=y_root[:, g % 2, u:u + 1], op0=ALU.mult,
                                         op1=ALU.mult).then_inc(S["ystat_ready"], 1)

            def shift_h(g, u, b):
                dve.wait_ge(S["mul_ready"], 2 * g + u + 1)
                y = y_sb[:, g % 2, u, :]
                dve.tensor_tensor(y, y, batch_row(ADD, b), ALU.add).then_inc(S["h_ready"], 1)

            def silu_h(g, u):
                dve.wait_ge(S["tanh_ready"], 2 * g + u + 1)
                y = y_sb[:, g % 2, u, :]
                dve.scalar_tensor_tensor(out=y, in0=t_sb[:, u, :], scalar=1.0, in1=y, op0=ALU.add,
                                         op1=ALU.mult).then_inc(S["s_ready"], 1)

            def low_s(g, u, b):
                dve.wait_ge(S["sh_ready"], 2 * g + u + 1)
                dve.scalar_tensor_tensor(out=sT[:, 1, u, :, :].rearrange("p j c -> p (j c)"), in0=ps[:, ST_BANK, :],
                                         scalar=top_r[:, 3 + b:4 + b],
                                         in1=sT[:, 0, u, :, :].rearrange("p j c -> p (j c)"), op0=ALU.mult,
                                         op1=ALU.subtract).then_inc(S["sl_ready"], 1)

            done = [0]

            def link(ins):
                done[0] += 1
                ins.then_inc(S["setup_step"], 1)
                dve.wait_ge(S["setup_step"], done[0])

            front(0)
            dve.wait_ge(S["prm_T"], 1)
            dve.tensor_copy(cols[:, :], ps[:, 7, 0:NR]).then_inc(S["cols_ready"], 1)
            dve.wait_ge(S["cols_ready"], 1)
            dve.wait_ge(S["silu_ready"], 1)
            dve.scalar_tensor_tensor(out=silu2[:, :], in0=silu_t[:, :], scalar=1.0, in1=cols[:, 2 * C:NR],
                                     op0=ALU.add, op1=ALU.mult).then_inc(S["silu2_ready"], 1)

            def size_weight(n, raw, came, scaled):
                dve.wait_ge(came, 16)
                link(dve.tensor_reduce(size_c[:, :], raw, AX.X, ALU.max, apply_absolute_value=True))
                if scaled:
                    link(dve.tensor_tensor(size_c[:, :], size_c[:, :], cols[:, 0:C], ALU.mult))
                dve.tensor_reduce(stat[:, n:n + 1], size_c[:, :], AX.X, ALU.max,
                                  apply_absolute_value=True).then_inc(S["stat_ready"], 1)

            def size_all(n):
                dve.wait_ge(S["statT"], n + 1)
                dve.tensor_reduce(stat_m[:, :], ps[0:1, 7, 0:P], AX.X, ALU.max).then_inc(S["stat_max_done"], 1)

            def to_power(src, a, z):
                link(dve.tensor_scalar(pow2[:, a:z], src, 1e-30, None, ALU.max))
                link(dve.tensor_scalar(pow2[:, a:z].bitcast(I32), pow2[:, a:z].bitcast(I32), EXPONENT, None,
                                       ALU.bitwise_and))
                link(dve.reciprocal(top_r[:, a:z], pow2[:, a:z]))
                link(dve.tensor_scalar(top_r[:, a:z], top_r[:, a:z], TOP, None, ALU.mult))

            def scale_weight(n, inv):
                dve.wait_ge(S["stat_b"], n + 1)
                to_power(ps[:, 7, P:P + 1], n, n + 1)
                if inv is not None:
                    link(dve.tensor_scalar(norm_top[:, n, :], cols[:, 0:C], top_r[:, n:n + 1], None, ALU.mult))
                    link(dve.tensor_scalar(inv[:, :], pow2[:, n:n + 1], 1.0 / (TOP * Z_SCALE), None, ALU.mult))
                dve.memset(spot[:, 0, 0:1], 0.0).then_inc(S["scales_ready"], 1)

            size_weight(0, wk_raw, S["wk_in"], True)
            size_all(0)
            scale_weight(0, inv_k)
            for j in range(C):
                dve.wait_ge(S["wk_hi"], j + 1)
                last = dve.scalar_tensor_tensor(out=wk[:, 1, j, :], in0=wk_raw[:, j, :],
                                                scalar=norm_top[:, 0, j:j + 1], in1=wk[:, 0, j, :], op0=ALU.mult,
                                                op1=ALU.subtract)
            last.then_inc(S["wk_ready"], 1)
            for n in range(1, 4):
                front(n)
            link(dve.memset(ctx_bd[:, :, :, :], 0.0))
            for r in range(HC):
                last = dve.memset(ctx_bd[r * DH:(r + 1) * DH, :, r, DH:DH + 1], 1.0)
            link(last)
            link(dve.memset(z256[:, :], Z_SCALE))
            dve.wait_ge(S["bias_ready"], 1)

            def bound_silu():
                dve.wait_ge(S["row_step"], 6)
                link(dve.tensor_reduce(bound[:, :], wide[0:B, SNG:SNB + 1, :], AX.X, ALU.max,
                                       apply_absolute_value=True))
                link(dve.scalar_tensor_tensor(out=bound[:, 0:1], in0=bound[:, 0:1], scalar=math.sqrt(D) * 1.01,
                                              in1=bound[:, 1:2], op0=ALU.mult, op1=ALU.add))
                dve.tensor_scalar(bound_d[:, :], ident[0:B, 0:B], bound[:, 0:1], None,
                                  ALU.mult).then_inc(S["bound_diag"], 1)

            def scale_silu():
                dve.wait_ge(S["bound_b"], 1)
                to_power(ps[:, 7, P:P + B], 3, 3 + B)
                for b in range(B):
                    link(dve.scalar_tensor_tensor(out=inv_o[:, b:b + 1], in0=pow2[:, 3 + b:4 + b],
                                                  scalar=0.5 / TOP ** 2, in1=pow2[:, 2:3], op0=ALU.mult,
                                                  op1=ALU.mult))
                dve.memset(spot[:, 1, 0:1], 0.0).then_inc(S["scales_ready"], 1)

            for b in range(B):
                first = b * NP
                dve.wait_ge(S["acc_cleared"], 2 * b + 1)

                for u in range(2):
                    stats_x(first + 4, u)
                for i in range(NP):
                    g = first + i
                    ends, roots, comes = 0 < i and i + 3 < NP, i + 4 < NP, i + 5 < NP
                    if ends:
                        square_x(g + 3, 2)
                    if b > 0 and i == 1:
                        dve.wait_ge(S["o_done"], 2 * first)
                    if b > 0 and i == 2:
                        dve.wait_ge(S["stored"], 16 * first)
                    keep_k(g, i, 0)
                    if ends:
                        root_x(g + 3, 2)
                    keep_k(g, i, 1)
                    if ends:
                        finish_x(g + 3)
                    if roots:
                        aggregate_x(g + 4)
                    running_max(g, i, 0)
                    if roots:
                        halve_x(g + 4)
                    running_max(g, i, 1)
                    if roots:
                        guess_x(g + 4)
                    if comes:
                        stats_x(g + 5, 0)
                    if roots:
                        square_x(g + 4, 0)
                    if comes:
                        stats_x(g + 5, 1)
                    if roots:
                        root_x(g + 4, 0)
                        square_x(g + 4, 1)
                        root_x(g + 4, 1)
                dve.wait_ge(S["kT_done"], b + 1)
                dve.tensor_reduce(m_col[:, :], ps[:, M_BANK:M_BANK + 2, :].rearrange("p u (j t) -> p j u t", j=C),
                                  AX.XY, ALU.max).then_inc(S["ctx_step"], 1)
                dve.wait_ge(S["ctx_step"], 6 * b + 1)
                dve.tensor_tensor(m_diag[:, :, :], ident[:, :].rearrange("p (o c) -> p o c", o=1).broadcast_to([P, C, P]),
                                  m_col[:, :].rearrange("p (j o) -> p j o", o=1).broadcast_to([P, C, P]),
                                  ALU.mult).then_inc(S["mdiag_ready"], 1)
                dve.wait_ge(S["mrow_done"], b + 1)
                dve.tensor_scalar(m_row, ps[:, M_BANK, :], EK_SHIFT, None, ALU.subtract).then_inc(S["mrow_ready"], 1)
                dve.wait_ge(S["acc_cleared"], 2 * b + 2)
                split_ek(first)
                split_ek(first + 1)
                if b + 1 < B:
                    for i in range(2, NP):
                        split_ek(first + i)
                        if i in (3, 5):
                            front(first + NP + i // 2 - 1)
                        if i == 2:
                            size_weight(1, wq_raw, S["wq_in"], True)
                        elif i == 3:
                            size_all(1)
                        elif i == 4:
                            scale_weight(1, inv_q)
                            size_weight(2, wo_raw, S["wo_in"], False)
                        elif i == 5:
                            size_all(2)
                        elif i == 6:
                            scale_weight(2, None)
                            bound_silu()
                    scale_silu()
                else:
                    with dve.Fori(2, NP) as i:
                        split_ek(i + first)
                if b == 0:
                    dve.wait_ge(S["bias_ready"], 3)
                dve.wait_ge(S["g_pair"], first + NP)
                dve.wait_ge(S["s_done"], first + NP)
                dve.tensor_copy(gT[:, 2:4, :], ps[:, G_BANK + 2:G_BANK + 4, :]).then_inc(S["gT_ready"], 1)
                def start_q(t):
                    keep_q(first + t // 2, t % 2)
                    max_q(first + t // 2, t % 2)

                start_q(0)
                dve.wait_ge(S["s_sum"], b + 1)
                dve.reciprocal(r_s[:, :], ps[:, CTX_BANK + 1, 0:C]).then_inc(S["ctx_step"], 1)
                dve.wait_ge(S["ctx_step"], 6 * b + 2)
                dve.wait_ge(S["ctx_done"], b + 1)
                for r in range(HC):
                    q = slice(r * DH, (r + 1) * DH)
                    last = dve.tensor_tensor(
                        ctx_bd[q, :, r, 0:DH], ps[q, CTX_BANK, :].rearrange("p (j c) -> p j c", j=C)[:, :, q],
                        r_s[q, :].rearrange("p (j o) -> p j o", o=1).broadcast_to([DH, C, DH]), ALU.mult)
                    last.then_inc(S["ctx_step"], 1)
                dve.wait_ge(S["ctx_step"], 6 * b + 6)
                for r in range(HC):
                    q = slice(r * DH, (r + 1) * DH)
                    last = dve.tensor_tensor(
                        ctx_bd[q, :, r, 0:DH], ctx_bd[q, :, r, 0:DH],
                        wide[q, 2, :].rearrange("p (j c) -> p j c", j=C)[:, :, q], ALU.add)
                    last.then_inc(S["ctx_ready"], 1)

                def step(i, g, u):
                    i1, g1, u1 = ahead(i, g, u, 1)
                    i2, g2, u2 = ahead(i, g, u, 2)
                    i3, g3, u3 = ahead(i, g, u, 3)
                    i5, g5, u5 = ahead(i, g, u, 5)
                    i0, g0, u0 = ahead(i, g, u, -1)
                    roots = lives(i2)
                    more_q = lives(i5) and not (isinstance(i5, int) and i5 < 2)
                    if lives(i1):
                        finish_y(g1, u1)
                    if roots:
                        aggregate_y(g2, u2)
                    if lives(i0):
                        low_s(g0, u0, b)
                    if roots:
                        halve_y(g2, u2)
                    if more_q:
                        keep_q(g5, u5)
                    if roots:
                        guess_y(g2, u2)
                    if lives(i1):
                        shift_h(g1, u1, b)
                    if roots:
                        square_y(g2, u2, 0)
                    if more_q:
                        max_q(g5, u5)
                    if roots:
                        root_y(g2, u2, 0)
                    if lives(i3):
                        invert_sum(g3, u3)
                    if roots:
                        square_y(g2, u2, 1)
                    if lives(i3):
                        keep_y(g3, u3)
                    if roots:
                        root_y(g2, u2, 1)
                    if lives(i1):
                        silu_h(g1, u1)
                    if roots:
                        square_y(g2, u2, 2)
                    if lives(i3):
                        stats_y(g3, u3)
                    if roots:
                        root_y(g2, u2, 2)

                start_q(1)
                start_q(2)
                step(-2, first - 2, 1)
                start_q(3)
                step(-1, first - 1, 0)
                over_tiles(dve, b, 2, step)
                for i in range(NP - 3, NP):
                    step(i, first + i, 0)
                    step(i, first + i, 1)
                low_s(first + NP - 1, 1, b)
                if b + 1 < B:
                    front(first + NP + 2)
                    front(first + NP + 3)
        @block.tensor
        def _(pe):
            def three(out_ap, high, low, w, ready=None):
                n = 0
                for s, part in ((0, high), (1, high), (0, low)):
                    for j in range(C):
                        last = pe.matmul(out_ap, part(j), w[:, s, j, :], start=(n == 0), stop=(n == 3 * C - 1))
                        n += 1
                last.then_inc(ready, 1)

            def turn_z(g, i):
                pe.wait_ge(S["zl_ready"], g + 1)
                for u in range(2):
                    for s, z in enumerate((zh, zl)):
                        for j in range(C):
                            last = pe.transpose(ps16[:, Q_BANK + u, (s * C + j) * P:(s * C + j + 1) * P],
                                                z[:, 2 * i + u, j * P:(j + 1) * P], ident16[:, :])
                    last.then_inc(S["t_done"], 1)

            def product_k(g, i, u):
                pe.wait_ge(S["zT_ready"], 2 * g + u + 1)
                if not starts(g, 2):
                    pe.wait_ge(S["k_ready"], 2 * g + u - 3)
                bank = K_BANK + 2 * (g % 2) + u
                three(ps[:, bank, :], lambda j: zT[:, 2 * i + u, 0, j, :], lambda j: zT[:, 2 * i + u, 1, j, :], wk,
                      S["k_done"])

            def product_q(g, i, u):
                if not starts(g, 1):
                    pe.wait_ge(S["q_evac"], 2 * g + u - 1)
                three(ps[:, Q_BANK + u, :], lambda j: zT[:, 2 * i + u, 0, j, :], lambda j: zT[:, 2 * i + u, 1, j, :],
                      wq, S["q_done"])

            def product_g(g, i, start, stop):
                pe.wait_ge(S["ekl_ready"], g + 1)
                for u in range(2):
                    for c in range(C):
                        for n, (z, e) in enumerate(((zh, ekh), (zh, ekl), (zl, ekh))):
                            last = pe.matmul(ps[:, G_BANK + c, :], z[:, 2 * i + u, c * P:(c + 1) * P],
                                             e[:, g % 2, u, :], start=start and u == 0 and n == 0,
                                             stop=stop and u == 1 and n == 2)
                last.then_inc(S["g_pair"], 1)
                return last

            def turn_q(g, a, u):
                pe.wait_ge(S["qexp_done"], 2 * g + u + 1)
                if not starts(g, 1):
                    pe.wait_ge(S["eqT_ready"], 2 * g + u - 1)
                for j in range(C):
                    last = pe.transpose(ps[:, EQT_BANK + u, j * P:(j + 1) * P], q_sb[:, a, u, j * P:(j + 1) * P],
                                        ident[:, :])
                last.then_inc(S["eqT_done"], 1)

            def product_y(g, u):
                pe.wait_ge(S["eqT_ready"], 2 * g + u + 1)
                if not (starts(g, 1) and u == 0):
                    pe.wait_ge(S["y_ready"], 2 * g + u)
                for j in range(C):
                    last = pe.matmul(ps[:, Y_BANK + j // 2, (j % 2) * YW:(j % 2 + 1) * YW], eqT[:, u, j, :],
                                     ctx_bd[:, j, :, :].rearrange("p h d -> p (h d)"), start=True, stop=True)
                last.then_inc(S["y_done"], 1)

            def turn_s(g, a, u):
                pe.wait_ge(S["s_ready"], 2 * g + u + 1)
                if not (starts(g, 1) and u == 0):
                    pe.wait_ge(S["sl_ready"], 2 * g + u)
                for j in range(C):
                    last = pe.transpose(ps[:, ST_BANK, j * P:(j + 1) * P], y_sb[:, a, u, j * P:(j + 1) * P],
                                        ident[:, :])
                last.then_inc(S["sT_done"], 1)

            def product_out(g, u):
                pe.wait_ge(S["sl_ready"], 2 * g + u + 1)
                if not (starts(g, 1) and u == 0):
                    pe.wait_ge(S["fin_ready"], 2 * g + u)
                three(ps[:, OUT_BANK, :], lambda j: sT[:, 0, u, j, :], lambda j: sT[:, 1, u, j, :], wo, S["o_done"])

            def turn_size(n):
                pe.wait_ge(S["stat_ready"], n + 1)
                pe.transpose(ps[0:1, 7, 0:P], stat[:, n:n + 1], ident[:, :]).then_inc(S["statT"], 1)

            def spread_size(n):
                pe.wait_ge(S["stat_max_done"], n + 1)
                pe.matmul(ps[:, 7, P:P + 1], ones[0:1, :], stat_m[:, :], start=True, stop=True).then_inc(S["stat_b"], 1)

            def bias_product(n, w, bank):
                for j in range(C):
                    pe.matmul(ps[:, bank, :], cols[:, C + j:C + j + 1].broadcast_to([P, P]), w[:, j, :],
                              start=(j == 0), stop=False)
                pe.matmul(ps[:, bank, :], ones[0:1, :], wide[0:1, n, :], start=False,
                          stop=True).then_inc(S["bias_done"], 1)

            pe.wait_ge(S["const_ready"], 4)
            pe.wait_ge(S["prm_in"], 48)
            pe.transpose(ps[:, 7, 0:NR], prm[:, :], ident[0:NR, 0:NR]).then_inc(S["prm_T"], 1)
            pe.wait_ge(S["cols_ready"], 1)
            pe.wait_ge(S["wk_in"], 16)
            pe.wait_ge(S["bias_in"], 48)
            turn_size(0)
            spread_size(0)
            bias_product(0, wk_raw, 6)
            turn_z(0, 0)
            pe.wait_ge(S["wk_ready"], 1)

            for b in range(B):
                first = b * NP
                def step_a(i, g, more=True):
                    product_k(g, i, 0)
                    if more:
                        pe.wait_ge(S["zT_ready"], 2 * g + 2)
                        turn_z(g + 1, i + 1)
                    product_k(g, i, 1)

                if b == 0:
                    step_a(0, 0)
                    step_a(1, 1)
                    with pe.Fori(2, NP - 1) as i:
                        step_a(i, i)
                else:
                    with pe.Fori(1, NP - 1) as i:
                        step_a(i, i + first)
                step_a(NP - 1, first + NP - 1, False)
                pe.wait_ge(S["zT_ready"], 2 * (first + NP))
                if b == 0:
                    pe.wait_ge(S["silu2_ready"], 1)
                    pe.wait_ge(S["emb_in"], 32)
                    pe.wait_ge(S["k_ready"], 2 * NP - 2)
                    for h in range(2):
                        for j in range(C):
                            e = emb_a if j < 2 else emb_b2
                            last = pe.matmul(ps[0:B, K_BANK + h, :], silu2[:, j:B * C:C],
                                             e[:, j % 2, h * D:(h + 1) * D], start=(j == 0), stop=(j == C - 1))
                    last.then_inc(S["emb_done"], 1)
                else:
                    product_q(first, 0, 0)
                pe.wait_ge(S["kmax_done"], 2 * (first + NP))
                for u in range(2):
                    for j in range(C):
                        last = pe.transpose(ps[:, M_BANK + u, j * P:(j + 1) * P], acc[:, u, j * P:(j + 1) * P],
                                            ident[:, :])
                last.then_inc(S["kT_done"], 1)
                if b > 0:
                    product_q(first, 0, 1)
                pe.wait_ge(S["mdiag_ready"], b + 1)
                pe.matmul(ps[:, M_BANK, :], ones[:, :], m_diag[:, :, :].rearrange("p j c -> p (j c)"), start=True,
                          stop=True).then_inc(S["mrow_done"], 1)
                if b == 0:
                    pe.wait_ge(S["wv_in"], 16)
                    pe.wait_ge(S["k_ready"], 2 * NP)
                    bias_product(2, wv, K_BANK + 2)
                pe.wait_ge(S["k_ready"], 2 * (first + NP))
                if b == 0:
                    pe.wait_ge(S["bias_ready"], 2)
                    pe.wait_ge(S["emb_kept"], 1)
                product_g(first, 0, True, False)
                if b == 0:
                    for i in range(1, NP - 1):
                        product_g(i, i, False, False)
                        if i == 2:
                            turn_size(1)
                        elif i == 3:
                            spread_size(1)
                            bias_product(1, wq_raw, 6)
                        elif i == 4:
                            turn_size(2)
                        elif i == 5:
                            spread_size(2)
                else:
                    with pe.Fori(1, NP - 1) as i:
                        product_g(i + first, i, False, False)
                product_g(first + NP - 1, NP - 1, False, True)
                if b == 0:
                    pe.wait_ge(S["bound_diag"], 1)
                    pe.matmul(ps[:, 7, P:P + B], ones[0:B, :], bound_d[:, :], start=True,
                              stop=True).then_inc(S["bound_b"], 1)
                    pe.wait_ge(S["w_ready"], 1)
                    product_q(first, 0, 0)
                else:
                    product_q(first + 1, 1, 0)
                pe.wait_ge(S["s_done"], first + NP)
                pe.wait_ge(S["scales_ready"], 4)
                for j in range(C):
                    for u in range(2):
                        last = pe.matmul(ps[:, CTX_BANK + 1, j:j + 1], acc[:, u, j * P:(j + 1) * P], z256[:, :],
                                         start=(u == 0), stop=(u == 1))
                last.then_inc(S["s_sum"], 1)
                pe.wait_ge(S["gT_ready"], 2 * b + 2)
                for j in range(C):
                    for c in range(C):
                        last = pe.matmul(ps[:, CTX_BANK, j * P:(j + 1) * P], gT[:, c, j * P:(j + 1) * P],
                                         wv[:, c, j * P:(j + 1) * P], start=(c == 0), stop=(c == C - 1))
                last.then_inc(S["ctx_done"], 1)
                if b == 0:
                    product_q(first, 0, 1)
                    product_q(first + 1, 1, 0)
                turn_q(first, 0, 0)
                product_q(first + 1, 1, 1)
                turn_q(first, 0, 1)
                pe.wait_ge(S["ctx_ready"], HC * (b + 1))
                product_y(first, 0)
                product_q(first + 2, 2, 0)
                turn_q(first + 1, 1, 0)
                product_y(first, 1)
                product_y(first + 1, 0)
                if b == 0:
                    pe.wait_ge(S["w_ready"], 2)

                def step_c(i, g, a, u):
                    i3, g3, u3 = ahead(i, g, u, 3)
                    i5, g5, u5 = ahead(i, g, u, 5)
                    a3 = (a + (u + 3) // 2) % 2
                    i0, g0, u0 = ahead(i, g, u, -1)
                    if lives(i3):
                        turn_q(g3, a3, u3)
                    if lives(i5):
                        product_q(g5, i5, u5)
                    if lives(i):
                        turn_s(g, a, u)
                    if lives(i3):
                        product_y(g3, u3)
                    if lives(i0):
                        product_out(g0, u0)

                for u in range(2):
                    step_c(0, first, 0, u)
                with pe.Fori(0, (NP - 4) // 2) as n:
                    for p in range(2):
                        for u in range(2):
                            step_c(n * 2 + (1 + p), n * 2 + (first + 1 + p), 1 - p, u)
                for i in range(NP - 3, NP + 1):
                    for u in range(2):
                        if (i, u) == (NP - 1, 0) and b + 1 < B:
                            pe.wait_ge(S["q_evac"], 2 * (first + NP))
                            turn_z(first + NP, 0)
                        step_c(i, first + i, i % 2, u)
                        if (i, u) == (NP - 1, 0) and b + 1 < B:
                            pe.wait_ge(S["y_ready"], 2 * (first + NP))
                            product_k(first + NP, 0, 0)
                        if (i, u) == (NP - 1, 1) and b + 1 < B:
                            pe.wait_ge(S["zT_ready"], 2 * (first + NP) + 2)
                            turn_z(first + NP + 1, 1)
                if b + 1 < B:
                    product_k(first + NP, 0, 1)




_INS = ["x", "cond_1024"] + ["L0_cond_" + n for n in (
    "norm_g", "norm_b", "Wq", "bq", "Wk", "bk", "Wv", "bv", "emb_W", "emb_b", "sn_g", "sn_b", "out_W", "out_b")]


def kernel(**inputs):
    import numpy as np
    from concourse import bacc
    from concourse.bass_utils import run_bass_kernel_spmd

    nc = bacc.Bacc("TRN2", target_bir_lowering=False, num_devices=1)
    arrays, args = {}, []
    for name in _INS:
        a = np.ascontiguousarray(inputs[name])
        arrays[f"in_{name}_dram"] = a
        args.append(nc.dram_tensor(f"in_{name}_dram", a.shape, mybir.dt.from_np(a.dtype), kind="ExternalInput").ap())
    shape = arrays["in_x_dram"].shape
    args.append(nc.dram_tensor("out_0_dram", shape, F32, kind="ExternalOutput").ap())
    linear_attention_block(nc, *args)
    r = run_bass_kernel_spmd(nc, [arrays], core_ids=[0])
    return r.results[0]["out_0_dram"]
```

```python
import math
from contextlib import ExitStack

import concourse.bass as bass
from concourse import mybir

F32 = mybir.dt.float32
F16 = mybir.dt.float16
I32 = mybir.dt.int32
ALU = mybir.AluOpType
ACT = mybir.ActivationFunctionType
AX = mybir.AxisListType

P = 128
HEADS = 16
EPS = 1e-5
Z_SCALE = 256.0
EK_SHIFT = 15 * math.log(2.0)
TOP = 8192.0
EXPONENT = 0x7F800000
GUESS = 0x5F3759DF - (1 << 22) - (1 << 31)
X_STEPS = 16
Y_STEPS = 9
LOWEST = -3.4028234e38


def linear_attention_block(nc, x, cond, norm_g, norm_b, Wq, bq, Wk, bk, Wv, bv, emb_W, emb_b,
                           sn_g, sn_b, out_W, out_b, out):
    B, T, D = x.shape
    C = D // P
    DH = D // HEADS
    HC = P // DH
    NP = T // (2 * P)
    YW = HC * (DH + 1)
    NR = (2 + B) * C

    x_v = x.rearrange("b (i p u) c -> (b i) p u c", p=P, u=2)
    out_v = out.rearrange("b (i p u) c -> (b i) p u c", p=P, u=2)

    def chunked(w):
        return w.rearrange("(j p) n -> p j n", p=P)

    def rows(v):
        return v.rearrange("(j p) -> j p", p=P)

    with ExitStack() as ctx:
        def sb(name, shape, dt=F32):
            return ctx.enter_context(nc.sbuf_tensor(name, shape, dt))

        def sem(name):
            return ctx.enter_context(nc.semaphore(name))

        wk = sb("wk", [P, 2, C, D], F16)
        wq = sb("wq", [P, 2, C, D], F16)
        wo = sb("wo", [P, 2, C, D], F16)
        wv = sb("wv", [P, C, D])
        NB = 3 + 4 * B
        wide = sb("wide", [P, NB, D])
        kb_row, qb_row, vb_row = wide[:, 0, :], wide[:, 1, :], wide[:, 2, :]

        def batch_row(kind, b):
            return wide[:, 3 + 4 * b + kind, :]

        MUL, ADD, GOB, GATE = range(4)

        ident = sb("ident", [P, P])
        ident16 = sb("ident16", [P, P], F16)
        ones = sb("ones", [P, P])
        z256 = sb("z256", [P, 1])
        cols = sb("cols", [P, NR])
        prm = sb("prm", [NR, P])
        silu2 = sb("silu2", [P, B * C])
        silu_t = sb("silu_t", [P, B * C])
        size_c = sb("size_c", [P, C])
        stat = sb("stat", [P, 3])
        stat_m = sb("stat_m", [1, 1])
        norm_top = sb("norm_top", [P, 2, C])
        pow2 = sb("pow2", [P, 3 + B])
        top_r = sb("top_r", [P, 3 + B])
        bound = sb("bound", [B, 2])
        bound_d = sb("bound_d", [B, B])
        inv_k, inv_q = sb("inv_k", [P, 1]), sb("inv_q", [P, 1])
        inv_o = sb("inv_o", [P, B])

        zh = sb("zh", [P, 2 * NP, D], F16)
        zl = sb("zl", [P, 2 * NP, D], F16)
        zT = sb("zT", [P, 2 * NP, 2, C, P], F16)
        k_all = sb("k_all", [P, NP, 2, D])
        x_in = sb("x_in", [P, 4, 2, D])
        z_sb = sb("z_sb", [P, 2, 2, D])
        bn6 = sb("bn6", [P, 2, 6])
        mv = sb("mv", [P, 2, 2])
        half_v = sb("half_v", [P, 2])
        root = sb("root", [P, 2, 2])
        root_t = sb("root_t", [P, 2])
        z_nmr = sb("z_nmr", [P, 2, 2])
        acc = sb("acc", [P, 2, D])
        m_col = sb("m_col", [P, C])
        m_diag = sb("m_diag", [P, C, P])
        m_row = m_diag[:, :, :].rearrange("p j c -> p (j c)")
        ek = sb("ek", [P, 2, 2, D])
        ekh, ekl = (x_in[:, n, :, :].rearrange("p u c -> p (u c)").bitcast(F16)
                    .rearrange("p (a u c) -> p a u c", a=2, u=2) for n in (2, 3))
        r_s = sb("r_s", [P, C])
        ctx_bd = sb("ctx_bd", [P, C, HC, DH + 1])
        q_sb = sb("q_sb", [P, 2, 2, D])
        q_max = sb("q_max", [P, 2, 2, HEADS])
        eqT = sb("eqT", [P, 2, C, P])
        r_q = sb("r_q", [P, 2, HEADS])
        y_bn6 = sb("y_bn6", [P, 2, 6])
        y_mv = sb("y_mv", [P, 2, 2])
        y_half_v = sb("y_half_v", [P, 2])
        y_root = sb("y_root", [P, 2, 2])
        y_root_t = sb("y_root_t", [P, 2])
        spot = sb("spot", [P, 2, 1])
        y_nmr = sb("y_nmr", [P, 2, 2])

        gT = ek[:, :, :, :].rearrange("p a u c -> p (a u) c")
        y_sb = ek
        spare = k_all[:, :, :, :].rearrange("p i u c -> p (i u c)")
        PAIR = 2 * D
        t_sb = spare[:, 0:PAIR].rearrange("p (u c) -> p u c", u=2)
        sT = spare[:, PAIR:2 * PAIR].bitcast(F16).rearrange("p (s u j c) -> p s u j c", s=2, u=2, j=C)
        fo = spare[:, 2 * PAIR:4 * PAIR].rearrange("p (a u c) -> p a u c", a=2, u=2)
        xr = spare[:, 4 * PAIR:8 * PAIR].rearrange("p (a u c) -> p a u c", a=4, u=2)
        wk_raw, wo_raw = (spare[:, n * C * D:(n + 1) * C * D].rearrange("p (j n) -> p j n", j=C) for n in range(2))
        wq_raw = wk_raw
        SNG, SNB, OUTB, COND, EMBB, EMB = 3, 4, 5, 6, 7, 9
        emb_front = ek[:, :, :, :].rearrange("p a u c -> p (a u) c").rearrange("p (j h) c -> p j (h c)", h=2)
        emb_back = q_sb[:, :, :, :].rearrange("p a u c -> p (a u) c").rearrange("p (j h) c -> p j (h c)", h=2)

        scratch = nc.dram_tensor("rows_scratch", [B, 4 * D], F32, kind="Internal").ap()

        ps = ctx.enter_context(nc.psum_tensor("ps", [P, 8, D], F32))
        ps16 = ps[:, :, :].bitcast(F16)
        Q_BANK, K_BANK, EQT_BANK, Y_BANK, OUT_BANK, ST_BANK = 0, 2, 2, 4, 6, 7
        G_BANK, M_BANK, CTX_BANK = 2, 6, 6

        names = """prm_in bias_in rows_in x_in_done wk_in wq_in wv_in wo_in emb_in const_ready prm_T cols_ready
            silu_ready silu2_ready emb_done emb_kept scr_out wide_in stat_ready statT stat_max_done
            stat_b bias_done bias_ready wk_hi w_scaled w_high wk_ready w_ready wv_ready row_step bound_diag bound_b
            scales_ready setup_step x_stats x_step stat_ready_z z_ready zh_ready zl_ready t_done zT_ready
            k_done k_ready kmax_done kT_done mdiag_ready mrow_done mrow_ready acc_cleared
            ksub_first exp_tile ekh_first ekl_first ksub_done exp_done ekh_ready ekl_ready s_done g_pair s_sum gT_ready
            ctx_done ctx_step ctx_ready
            q_done q_evac qmax_done qsub_done qexp_done eqT_done eqT_ready y_done y_ready y_stats y_step
            ystat_ready gated n_ready mul_ready h_ready tanh_ready s_ready sT_done sh_ready sl_ready o_done
            fin_ready xr_in xg_ready out_ready stored rq_step last_gated last_ready bd_cleared""".split()
        S = {n: sem(n) for n in names}

        block = ctx.enter_context(nc.Block())

        first_q = [0 if b == 0 else 2 for b in range(B)]

        def starts(g, n):
            return isinstance(g, int) and g < n

        def is_last(g, u):
            return isinstance(g, int) and (g, u) == (B * NP - 1, 1)

        def ahead(i, g, u, n):
            return i + (u + n) // 2, g + (u + n) // 2, (u + n) % 2

        def lives(i):
            return not isinstance(i, int) or 0 <= i < NP

        def over_tiles(eng, b, peel, step):
            first = b * NP
            for u in range(-1, 2 * peel):
                step(u // 2, first + u // 2, u % 2)
            with eng.Fori(peel, NP - 3) as i:
                for u in range(2):
                    step(i, i + first, u)

        def over_pairs(eng, b, peel, end, step):
            first = b * NP
            peeled = peel if b == 0 else 0
            for i in range(peeled):
                step(i, first + i)
            with eng.Fori(peeled, end) as i:
                step(i, i + first)

        @block.sync
        def _(sp):
            sp.dma_start(x_in[:, 0, :, :], x_v[0]).then_inc(S["x_in_done"], 16)
            sp.dma_start(wk_raw, chunked(Wk)).then_inc(S["wk_in"], 16)
            for n in range(1, 4):
                sp.wait_ge(S["x_in_done"], 16 * n)
                sp.dma_start(x_in[:, n, :, :], x_v[n]).then_inc(S["x_in_done"], 16)

            def load_x(g):
                sp.wait_ge(S["x_in_done"], 16 * g)
                if not starts(g, 4):
                    sp.wait_ge(S["z_ready"], 2 * g - 6)
                sp.dma_start(x_in[:, g % 4, :, :], x_v[g]).then_inc(S["x_in_done"], 16)

            def load_residual(g):
                if not starts(g, 1):
                    sp.wait_ge(S["xr_in"], 16 * g)
                sp.dma_start(xr[:, g % 4, :, :], x_v[g]).then_inc(S["xr_in"], 16)

            def store(g):
                if not starts(g, 1):
                    sp.wait_ge(S["stored"], 16 * g)
                if is_last(g, 1):
                    sp.wait_ge(S["out_ready"], 2 * g + 1)
                    sp.dma_start(out_v[g][:, 0, :], fo[:, g % 2, 0, :]).then_inc(S["stored"], 16)
                    sp.wait_ge(S["last_ready"], 1)
                    sp.dma_start(out_v[g][:, 1, :], fo[:, g % 2, 1, :]).then_inc(S["stored"], 16)
                else:
                    sp.wait_ge(S["out_ready"], 2 * g + 2)
                    sp.dma_start(out_v[g], fo[:, g % 2, :, :]).then_inc(S["stored"], 16)

            load_x(4)
            sp.dma_start(emb_front, chunked(emb_W)[:, 0:2, :]).then_inc(S["emb_in"], 16)
            load_x(5)
            sp.dma_start(emb_back, chunked(emb_W)[:, 2:4, :]).then_inc(S["emb_in"], 16)
            sp.dma_start(wv[:, :, :], chunked(Wv)).then_inc(S["wv_in"], 16)
            for b in range(B):
                first = b * NP
                for i in range(6, NP):
                    load_x(first + i)
                if b + 1 < B:
                    load_x(first + NP)
                    load_x(first + NP + 1)
                if b == 0:
                    sp.wait_ge(S["ksub_first"], 1)
                    sp.wait_ge(S["ksub_done"], 2)
                    sp.dma_start(wq_raw, chunked(Wq)).then_inc(S["wq_in"], 16)
                    sp.wait_ge(S["ksub_done"], 4)
                    sp.dma_start(wo_raw, chunked(out_W)).then_inc(S["wo_in"], 16)
                    sp.wait_ge(S["bound_diag"], 1)
                    sp.dma_start(scratch.rearrange("b (r n) -> b r n", n=D),
                                 wide[0:B, SNG:SNG + 4, :]).then_inc(S["scr_out"], 16)
                    sp.wait_ge(S["scr_out"], 16)
                    sp.dma_start(wide[:, 3:NB, :].rearrange("p n c -> p (n c)"),
                                 scratch.rearrange("b r -> (b r)").rearrange("(o r) -> o r", o=1)
                                 .broadcast_to([P, 4 * B * D])).then_inc(S["wide_in"], 16)
                sp.wait_ge(S["ksub_done"], first + NP)
                for i in range(4):
                    load_residual(first + i)
                if b + 1 < B:
                    sp.wait_ge(S["g_pair"], first + NP)
                    load_x(first + NP + 2)
                    load_x(first + NP + 3)
                    load_x(first + NP + 4)
                    load_x(first + NP + 5)

                def step(i, g):
                    store(g)
                    load_residual(g + 4)

                over_pairs(sp, b, 1, NP - 4, step)
                for i in range(NP - 4, NP):
                    store(first + i)
            sp.wait_ge(S["stored"], 16 * B * NP + 16)

        @block.gpsimd
        def _(pool):
            pool.memset(ident[:, :], 0.0).then_inc(S["const_ready"], 1)
            pool.memset(ones[:, :], 1.0).then_inc(S["const_ready"], 1)
            pool.wait_ge(S["const_ready"], 2)
            pool.affine_select(out=ident[:, :], in_=ident[:, :], compare_op=ALU.not_equal, fill=1.0, base=0,
                               pattern=[[-1, P]], channel_multiplier=1).then_inc(S["const_ready"], 1)
            pool.wait_ge(S["const_ready"], 3)
            pool.tensor_copy(ident16[:, :], ident[:, :]).then_inc(S["const_ready"], 1)
            pool.memset(z256[:, :], Z_SCALE).then_inc(S["bd_cleared"], 1)
            pool.memset(ctx_bd[:, :, :, :], 0.0).then_inc(S["bd_cleared"], 1)
            for r in range(HC):
                pool.wait_ge(S["bd_cleared"], 2 + r)
                pool.memset(ctx_bd[r * DH:(r + 1) * DH, :, r, DH:DH + 1], 1.0).then_inc(S["bd_cleared"], 1)
            pool.wait_ge(S["bd_cleared"], 2 + HC)
            pool.memset(acc[:, :, :], LOWEST).then_inc(S["acc_cleared"], 1)

            def low_z(g, i):
                pool.wait_ge(S["zh_ready"], g + 1)
                pool.tensor_tensor(zl[:, bass.ts(i, 2), :], z_sb[:, g % 2, :, :], zh[:, bass.ts(i, 2), :],
                                   ALU.subtract).then_inc(S["zl_ready"], 1)

            def modulation_rows():
                def row(n):
                    return wide[0:B, n, :]

                def link(n, out_row, a, c, op):
                    pool.tensor_tensor(out_row, a, c, op).then_inc(S["row_step"], 1)
                    pool.wait_ge(S["row_step"], n)

                pool.wait_ge(S["rows_in"], 80)
                pool.wait_ge(S["emb_kept"], 1)
                link(1, wide[0:B, EMB:EMB + 2, :], wide[0:B, EMB:EMB + 2, :], wide[0:B, EMBB:EMBB + 2, :], ALU.add)
                link(2, row(EMB), row(EMB), ones[0:B, 0:1].broadcast_to([B, D]), ALU.add)
                link(3, row(SNG), row(SNG), row(EMB), ALU.mult)
                link(4, row(SNB), row(SNB), row(EMB), ALU.mult)
                link(5, row(SNB), row(SNB), row(EMB + 1), ALU.add)
                link(6, row(OUTB), row(OUTB), row(COND), ALU.mult)

            def sub_max(g, i):
                if not starts(g, 2):
                    pool.wait_ge(S["s_done"], g - 1)
                    pool.wait_ge(S["ekl_ready"], g - 1)
                pool.tensor_tensor(ek[:, g % 2, :, :], k_all[:, i, :, :],
                                   m_row.rearrange("p (o c) -> p o c", o=1).broadcast_to([P, 2, D]),
                                   ALU.subtract).then_inc(S["ksub_done"], 1)

            def split_low(w, raw, n):
                pool.wait_ge(S["w_high"], n)
                pool.tensor_tensor(w[:, 1, :, :], raw, w[:, 0, :, :], ALU.subtract).then_inc(S["w_ready"], 1)

            def sub_q_max(g, u):
                pool.wait_ge(S["qmax_done"], 2 * g + u + 1)
                q = q_sb[:, g % 2, u, :].rearrange("p (h d) -> p h d", d=DH)
                m = q_max[:, g % 2, u, :].rearrange("p (h o) -> p h o", o=1)
                pool.tensor_tensor(q, q, m.broadcast_to([P, HEADS, DH]), ALU.subtract).then_inc(S["qsub_done"], 1)

            def modulate(g, u, b):
                pool.wait_ge(S["n_ready"], 2 * g + u + 1)
                y = y_sb[:, g % 2, u, :]
                pool.tensor_tensor(y, y, batch_row(MUL, b), ALU.mult).then_inc(S["mul_ready"], 1)

            def residual(g, u, b):
                pool.wait_ge(S["xr_in"], 16 * g + 16)
                r = xr[:, g % 4, u, :]
                pool.tensor_tensor(r, r, batch_row(GOB, b), ALU.add).then_inc(S["xg_ready"], 1)

            def add_residual(g, u, b):
                pool.wait_ge(S["fin_ready"], 2 * g + u + 1)
                pool.tensor_tensor(fo[:, g % 2, u, :], fo[:, g % 2, u, :], batch_row(GATE, b),
                                   ALU.mult).then_inc(S["gated"], 1)
                pool.wait_ge(S["wide_in"], 16)
                pool.wait_ge(S["gated"], 2 * g + u + 1)
                pool.wait_ge(S["xg_ready"], 2 * g + u + 1)
                pool.tensor_tensor(fo[:, g % 2, u, :], fo[:, g % 2, u, :], xr[:, g % 4, u, :],
                                   ALU.add).then_inc(S["out_ready"], 1)

            for b in range(B):
                first = b * NP
                if b == 0:
                    for n in range(3):
                        low_z(n, n)
                with pool.Fori(3, NP) as i:
                    low_z(i + first, i)
                pool.wait_ge(S["kT_done"], b + 1)
                pool.memset(acc[:, :, :], 0.0).then_inc(S["acc_cleared"], 1)
                pool.wait_ge(S["mrow_ready"], b + 1)
                if b > 0:
                    pool.wait_ge(S["ctx_done"], b)
                else:
                    pool.wait_ge(S["emb_done"], 2)
                pool.tensor_tensor(ek[:, first % 2, 1, :], k_all[:, 0, 1, :], m_row,
                                   ALU.subtract).then_inc(S["ksub_done"], 1)
                sub_max(first + 1, 1)
                if b + 1 < B:
                    for i in range(2, NP):
                        sub_max(first + i, i)
                        if i == 3:
                            modulation_rows()
                        if i in (5, 7):
                            low_z(first + NP + i // 2 - 2, i // 2 - 2)
                        if i == 6:
                            split_low(wq, wq_raw, 1)
                if b == 0:
                    split_low(wo, wo_raw, 2)
                else:
                    with pool.Fori(2, NP) as i:
                        sub_max(i + first, i)
                for t in range(4):
                    sub_q_max(first + t // 2, t % 2)
                    if t == 0 and b + 1 < B:
                        pool.wait_ge(S["s_sum"], b + 1)
                        pool.memset(acc[:, :, :], LOWEST).then_inc(S["acc_cleared"], 1)
                if b == 0:
                    pool.wait_ge(S["wide_in"], 16)

                def step(i, g, u):
                    i1, g1, u1 = ahead(i, g, u, 1)
                    i4, g4, u4 = ahead(i, g, u, 4)
                    i0, g0, u0 = ahead(i, g, u, -2)
                    if lives(i4) and not (isinstance(i4, int) and i4 < 2):
                        sub_q_max(g4, u4)
                    if lives(i1):
                        modulate(g1, u1, b)
                    if lives(i):
                        residual(g, u, b)
                    if lives(i0) and not is_last(g0, u0):
                        add_residual(g0, u0, b)

                over_tiles(pool, b, 1, step)
                for i in range(NP - 3, NP + 1):
                    step(i, first + i, 0)
                    if i == NP and b + 1 < B:
                        low_z(first + NP + 2, 2)
                    step(i, first + i, 1)

        @block.scalar
        def _(act):
            for n, v in enumerate((norm_g, norm_b)):
                act.dma_start(prm[n * C:(n + 1) * C, :], rows(v)).then_inc(S["prm_in"], 16)
            act.dma_start(prm[2 * C:NR, :], cond.rearrange("b (j p) -> (b j) p", p=P)).then_inc(S["prm_in"], 16)
            for n, v in enumerate((bk, bq, bv)):
                act.dma_start(wide[0:1, n, :], v.rearrange("(o c) -> o c", o=1)).then_inc(S["bias_in"], 16)
            for n, v in ((SNG, sn_g), (SNB, sn_b), (OUTB, out_b)):
                act.dma_start(wide[0:B, n, :], v.rearrange("(o c) -> o c", o=1).broadcast_to([B, D])
                              ).then_inc(S["rows_in"], 16)
            act.dma_start(wide[0:B, EMBB:EMBB + 2, :].rearrange("b n c -> b (n c)"),
                          emb_b.rearrange("(o c) -> o c", o=1).broadcast_to([B, 2 * D])).then_inc(S["rows_in"], 16)
            act.dma_start(wide[0:B, COND, :], cond).then_inc(S["rows_in"], 16)
            act.wait_ge(S["cols_ready"], 1)
            act.activation(silu_t[:, :], cols[:, 2 * C:NR], ACT.Tanh, scale=0.5).then_inc(S["silu_ready"], 1)

            def keep_out(g, u, b):
                act.wait_ge(S["o_done"], 2 * g + u + 1)
                if u == 0 and not starts(g, 2):
                    act.wait_ge(S["stored"], 16 * g - 16)
                act.activation(fo[:, g % 2, u, :], ps[:, OUT_BANK, :], ACT.Identity,
                               scale=inv_o[:, b:b + 1]).then_inc(S["fin_ready"], 1)

            def normalise_z(g):
                act.wait_ge(S["stat_ready_z"], g + 1)
                if not starts(g, 2):
                    act.wait_ge(S["zl_ready"], g - 1)
                for u in range(2):
                    act.activation(z_sb[:, g % 2, u, :], x_in[:, g % 4, u, :], ACT.Identity,
                                   bias=z_nmr[:, g % 2, u:u + 1],
                                   scale=root[:, g % 2, u:u + 1]).then_inc(S["z_ready"], 1)

            def high_z(g, i):
                act.wait_ge(S["z_ready"], 2 * g + 2)
                act.activation(zh[:, bass.ts(i, 2), :], z_sb[:, g % 2, :, :], ACT.Copy).then_inc(S["zh_ready"], 1)

            def keep_zT(g, i, u):
                if u == 0:
                    act.wait_ge(S["t_done"], 2 * g + 2)
                act.activation(zT[:, 2 * i + u, :, :, :].rearrange("p s j c -> p (s j c)"), ps16[:, Q_BANK + u, :],
                               ACT.Copy).then_inc(S["zT_ready"], 1)

            def exp_k(g, b):
                act.wait_ge(S["ksub_done"], g + 1)
                e = ek[:, g % 2, :, :]
                act.activation(e, e, ACT.Exp).then_inc(S["exp_done"], 1)
                act.wait_ge(S["exp_done"], g - b)
                if not starts(g, 2):
                    act.wait_ge(S["g_pair"], g - 1)
                act.activation(ekh[:, g % 2, :, :], e, ACT.Copy).then_inc(S["ekh_ready"], 1)

            def exp_q(g, u):
                act.wait_ge(S["qsub_done"], 2 * g + u + 1)
                q = q_sb[:, g % 2, u, :]
                act.activation(q, q, ACT.Exp).then_inc(S["qexp_done"], 1)

            def keep_eqT(g, u):
                act.wait_ge(S["eqT_done"], 2 * g + u + 1)
                if not starts(g, 1):
                    act.wait_ge(S["y_done"], 2 * g + u - 1)
                act.activation(eqT[:, u, :, :].rearrange("p j c -> p (j c)"), ps[:, EQT_BANK + u, :],
                               ACT.Copy).then_inc(S["eqT_ready"], 1)

            def normalise_y(g, u):
                act.wait_ge(S["ystat_ready"], 2 * g + u + 1)
                y = y_sb[:, g % 2, u, :]
                act.activation(y, y, ACT.Identity, bias=y_nmr[:, g % 2, u:u + 1],
                               scale=y_root[:, g % 2, u:u + 1]).then_inc(S["n_ready"], 1)

            def tanh_h(g, u):
                act.wait_ge(S["cols_ready"], 1)
                act.wait_ge(S["h_ready"], 2 * g + u + 1)
                act.activation(t_sb[:, u, :], y_sb[:, g % 2, u, :], ACT.Tanh, scale=0.5).then_inc(S["tanh_ready"], 1)

            def high_s(g, u, b):
                act.wait_ge(S["sT_done"], 2 * g + u + 1)
                if not starts(g, 1):
                    act.wait_ge(S["o_done"], 2 * g + u - 1)
                act.activation(sT[:, 0, u, :, :].rearrange("p j c -> p (j c)"), ps[:, ST_BANK, :], ACT.Identity,
                               scale=top_r[:, 3 + b:4 + b]).then_inc(S["sh_ready"], 1)

            def scale_split_high(w, raw, n):
                act.wait_ge(S["scales_ready"], n + 1)
                if n == 1:
                    act.wait_ge(S["bias_done"], 3)
                    for j in range(C):
                        act.activation(raw[:, j, :], raw[:, j, :], ACT.Identity,
                                       scale=norm_top[:, 1, j:j + 1]).then_inc(S["w_scaled"], 1)
                else:
                    act.activation(raw, raw, ACT.Identity, scale=top_r[:, 2:3]).then_inc(S["w_scaled"], 1)
                act.wait_ge(S["w_scaled"], C * min(n, 1) + (n - 1))
                act.activation(w[:, 0, :, :], raw, ACT.Copy).then_inc(S["w_high"], 1)

            normalise_z(0)
            high_z(0, 0)
            act.wait_ge(S["scales_ready"], 1)
            for j in range(C):
                act.activation(wk[:, 0, j, :], wk_raw[:, j, :], ACT.Identity,
                               scale=norm_top[:, 0, j:j + 1]).then_inc(S["wk_hi"], 1)
            keep_zT(0, 0, 0)
            keep_zT(0, 0, 1)
            normalise_z(1)
            high_z(1, 1)
            act.wait_ge(S["bias_done"], 1)
            act.activation(kb_row, ps[:, 6, :], ACT.Copy).then_inc(S["bias_ready"], 1)
            normalise_z(2)
            high_z(2, 2)
            for b in range(B):
                first = b * NP

                def step_a(i, g):
                    if not (b > 0 and isinstance(i, int)):
                        for u in range(2):
                            keep_zT(g + 1, i + 1, u)
                    normalise_z(g + 3)
                    high_z(g + 3, i + 3)

                step_a(0, first)
                with act.Fori(1, NP - 3) as i:
                    step_a(i, i + first)
                for i in range(NP - 2, NP):
                    for u in range(2):
                        keep_zT(first + i, i, u)
                if b == 0:
                    act.wait_ge(S["emb_done"], 2)
                    act.activation(wide[0:B, EMB:EMB + 2, :], ps[0:B, K_BANK:K_BANK + 2, :], ACT.Copy,
                                   scale=0.5).then_inc(S["emb_kept"], 1)
                e0, e1 = ek[:, first % 2, 0, :], ek[:, first % 2, 1, :]
                act.wait_ge(S["ksub_first"], b + 1)
                act.activation(e0, e0, ACT.Exp, scale=-1.0).then_inc(S["exp_tile"], 1)
                act.wait_ge(S["exp_tile"], 2 * b + 1)
                act.activation(ekh[:, first % 2, 0, :], e0, ACT.Copy).then_inc(S["ekh_first"], 1)
                act.wait_ge(S["ksub_done"], first + 1)
                act.activation(e1, e1, ACT.Exp).then_inc(S["exp_tile"], 1)
                act.wait_ge(S["exp_tile"], 2 * b + 2)
                act.activation(ekh[:, first % 2, 1, :], e1, ACT.Copy).then_inc(S["ekh_ready"], 1)
                exp_k(first + 1, b)
                if b + 1 < B:
                    for i in range(2, NP):
                        exp_k(first + i, b)
                        if i == 2:
                            act.wait_ge(S["bias_done"], 2)
                            act.activation(vb_row, ps[:, 7, :], ACT.Copy).then_inc(S["bias_ready"], 1)
                        if i == 3:
                            for j in range(C):
                                act.activation(wv[:, j, :], wv[:, j, :], ACT.Identity,
                                               scale=cols[:, j:j + 1]).then_inc(S["wv_ready"], 1)
                        if i == 5:
                            scale_split_high(wq, wq_raw, 1)
                        if i in (4, 6):
                            n = i // 2 - 2
                            normalise_z(first + NP + n)
                            act.wait_ge(S["g_pair"], first + n + 1)
                            high_z(first + NP + n, n)
                else:
                    with act.Fori(2, NP) as i:
                        exp_k(i + first, b)
                if b == 0:
                    act.wait_ge(S["bias_done"], 3)
                    act.activation(qb_row, ps[:, 6, :], ACT.Copy).then_inc(S["bias_ready"], 1)
                    scale_split_high(wo, wo_raw, 2)
                for u in range(first_q[b]):
                    exp_q(first, u)
                act.wait_ge(S["g_pair"], first + NP)
                act.wait_ge(S["s_done"], first + NP)
                act.activation(gT[:, 0:2, :], ps[:, G_BANK:G_BANK + 2, :], ACT.Copy).then_inc(S["gT_ready"], 1)
                if b == 0:
                    exp_q(first, 0)

                def step(i, g, u):
                    i0, g0, u0 = ahead(i, g, u, -1)
                    i9, g9, u9 = ahead(i, g, u, -2)
                    i1, g1, u1 = ahead(i, g, u, 1)
                    i3, g3, u3 = ahead(i, g, u, 3)
                    i4, g4, u4 = ahead(i, g, u, 4)
                    straight = isinstance(i, int)
                    early = straight and 2 * i + u <= 0
                    if lives(i0):
                        high_s(g0, u0, b)
                    if lives(i1) and not early:
                        normalise_y(g1, u1)
                    if lives(i3) and not (straight and 2 * i + u == 0):
                        keep_eqT(g3, u3)
                    if lives(i1) and early:
                        normalise_y(g1, u1)
                    if straight and 2 * i + u == -1:
                        keep_eqT(first + 1, 1)
                    if lives(i9) and not is_last(g9, u9):
                        keep_out(g9, u9, b)
                    if lives(i4) and not (isinstance(i4, int) and i4 < 2):
                        exp_q(g4, u4)
                    if lives(i1):
                        tanh_h(g1, u1)

                step(-2, first - 2, 1)
                if b == 0:
                    exp_q(first, 1)
                step(-1, first - 1, 0)
                exp_q(first + 1, 0)
                exp_q(first + 1, 1)
                over_tiles(act, b, 3, step)
                for i in range(NP - 3, NP + 1):
                    step(i, first + i, 0)
                    if b + 1 < B and i in (NP - 2, NP - 1):
                        n = i - (NP - 2)
                        keep_zT(first + NP + n, n, 0)
                        keep_zT(first + NP + n, n, 1)
                    if i == NP and b + 1 < B:
                        normalise_z(first + NP + 2)
                        high_z(first + NP + 2, 2)
                    step(i, first + i, 1)

        @block.vector
        def _(dve):
            def newton_square(y, half, tmp):
                return dve.scalar_tensor_tensor(out=tmp, in0=y, scalar=y, in1=half, op0=ALU.mult, op1=ALU.mult)

            def newton_root(y, tmp):
                return dve.scalar_tensor_tensor(out=y, in0=tmp, scalar=-1.5, in1=y, op0=ALU.add, op1=ALU.mult)

            def first_guess(y, half):
                return dve.tensor_scalar(y.bitcast(I32), half.bitcast(I32), -0.5, float(GUESS), ALU.mult, ALU.add)

            def stats_x(g, u):
                dve.wait_ge(S["x_in_done"], 16 * g + 16)
                if not starts(g, 1):
                    dve.wait_ge(S["x_step"], X_STEPS * g - X_STEPS + 2)
                dve.bn_stats(bn6[:, u, :], x_in[:, g % 4, u, :]).then_inc(S["x_stats"], 1)

            def aggregate_x(g):
                if not starts(g, 1):
                    dve.wait_ge(S["stat_ready_z"], g)
                dve.wait_ge(S["x_stats"], 2 * g + 2)
                dve.memset(root_t[:, :], 0.0)
                for u in range(2):
                    dve.bn_aggr(mv[:, u, :], bn6[:, u, :]).then_inc(S["x_step"], 1)

            def halve_x(g):
                dve.wait_ge(S["x_step"], X_STEPS * g + 2)
                dve.tensor_scalar(half_v[:, :], mv[:, :, 1], EPS, 0.5 / Z_SCALE ** 2, ALU.add,
                                  ALU.mult).then_inc(S["x_step"], 1)

            def guess_x(g):
                if not starts(g, 2):
                    dve.wait_ge(S["z_ready"], 2 * g - 2)
                dve.wait_ge(S["x_step"], X_STEPS * g + 3)
                first_guess(root[:, g % 2, :], half_v[:, :]).then_inc(S["x_step"], 1)

            def square_x(g, n):
                dve.wait_ge(S["x_step"], X_STEPS * g + 4 * n + 4)
                for u in range(2):
                    newton_square(root[:, g % 2, u:u + 1], half_v[:, u:u + 1],
                                  root_t[:, u:u + 1]).then_inc(S["x_step"], 1)

            def root_x(g, n):
                dve.wait_ge(S["x_step"], X_STEPS * g + 4 * n + 6)
                for u in range(2):
                    newton_root(root[:, g % 2, u:u + 1], root_t[:, u:u + 1]).then_inc(S["x_step"], 1)

            def finish_x(g):
                dve.wait_ge(S["x_step"], X_STEPS * g + 16)
                dve.scalar_tensor_tensor(out=z_nmr[:, g % 2, :], in0=mv[:, :, 0], scalar=-1.0,
                                         in1=root[:, g % 2, :], op0=ALU.mult,
                                         op1=ALU.mult).then_inc(S["stat_ready_z"], 1)

            def front_start(g):
                for u in range(2):
                    stats_x(g, u)
                aggregate_x(g)
                halve_x(g)
                guess_x(g)

            def front_end(g):
                for n in range(3):
                    square_x(g, n)
                    root_x(g, n)
                finish_x(g)

            def front(g):
                front_start(g)
                front_end(g)

            def keep_k(g, i, u):
                bank = K_BANK + 2 * (g % 2) + u
                dve.wait_ge(S["k_done"], 2 * g + u + 1)
                dve.scalar_tensor_tensor(out=k_all[:, i, u, :], in0=ps[:, bank, :], scalar=inv_k[:, 0:1],
                                         in1=kb_row, op0=ALU.mult, op1=ALU.add).then_inc(S["k_ready"], 1)

            def running_max(g, i, u):
                dve.wait_ge(S["k_ready"], 2 * g + u + 1)
                if not starts(g, 1):
                    dve.wait_ge(S["kmax_done"], 2 * g + u - 1)
                dve.tensor_tensor(acc[:, u, :], acc[:, u, :], k_all[:, i, u, :], ALU.max).then_inc(S["kmax_done"], 1)

            def split_ek(g):
                dve.wait_ge(S["ekh_ready"], g + 1)
                if not starts(g, 2):
                    dve.wait_ge(S["g_pair"], g - 1)
                dve.tensor_tensor(ekl[:, g % 2, :, :], ek[:, g % 2, :, :], ekh[:, g % 2, :, :],
                                  ALU.subtract).then_inc(S["ekl_ready"], 1)
                if not starts(g, 1):
                    dve.wait_ge(S["s_done"], g)
                dve.tensor_tensor(acc[:, :, :], acc[:, :, :], ek[:, g % 2, :, :], ALU.add).then_inc(S["s_done"], 1)

            def keep_q(g, u):
                dve.wait_ge(S["q_done"], 2 * g + u + 1)
                if not starts(g, 2):
                    dve.wait_ge(S["eqT_done"], 2 * g + u - 3)
                dve.scalar_tensor_tensor(out=q_sb[:, g % 2, u, :], in0=ps[:, Q_BANK + u, :], scalar=inv_q[:, 0:1],
                                         in1=qb_row, op0=ALU.mult, op1=ALU.add).then_inc(S["q_evac"], 1)

            def max_q(g, u):
                dve.wait_ge(S["q_evac"], 2 * g + u + 1)
                dve.tensor_reduce(q_max[:, g % 2, u, :], q_sb[:, g % 2, u, :].rearrange("p (h d) -> p h d", d=DH),
                                  AX.X, ALU.max).then_inc(S["qmax_done"], 1)

            both = ps[:, Y_BANK:Y_BANK + 2, 0:2 * YW].rearrange("p a (h d) -> p a h d", d=DH + 1)

            def invert_sum(g, u):
                dve.wait_ge(S["y_done"], 2 * g + u + 1)
                dve.reciprocal(r_q[:, u, :].rearrange("p (a h o) -> p a h o", a=2, o=1),
                               both[:, :, :, DH:DH + 1]).then_inc(S["rq_step"], 1)

            def keep_y(g, u):
                dve.wait_ge(S["rq_step"], 2 * g + u + 1)
                if not starts(g, 2):
                    dve.wait_ge(S["sT_done"], 2 * g + u - 3)
                dve.tensor_tensor(y_sb[:, g % 2, u, :].rearrange("p (a h d) -> p a h d", a=2, d=DH),
                                  both[:, :, :, 0:DH],
                                  r_q[:, u, :].rearrange("p (a h o) -> p a h o", a=2, o=1)
                                  .broadcast_to([P, 2, HEADS // 2, DH]), ALU.mult).then_inc(S["y_ready"], 1)

            def stats_y(g, u):
                dve.wait_ge(S["y_ready"], 2 * g + u + 1)
                dve.memset(spot[:, u, 0:1], 0.0)
                dve.bn_stats(y_bn6[:, u, :], y_sb[:, g % 2, u, :]).then_inc(S["y_stats"], 1)

            def y_at(g, u):
                return g * (2 * Y_STEPS) + u * Y_STEPS

            def aggregate_y(g, u):
                dve.wait_ge(S["y_stats"], 2 * g + u + 1)
                dve.memset(y_root_t[:, u:u + 1], 0.0)
                dve.bn_aggr(y_mv[:, u, :], y_bn6[:, u, :]).then_inc(S["y_step"], 1)

            def halve_y(g, u):
                dve.wait_ge(S["y_step"], y_at(g, u) + 1)
                dve.tensor_scalar(y_half_v[:, u:u + 1], y_mv[:, u, 1:2], EPS, 0.5, ALU.add,
                                  ALU.mult).then_inc(S["y_step"], 1)

            def guess_y(g, u):
                dve.wait_ge(S["y_step"], y_at(g, u) + 2)
                first_guess(y_root[:, g % 2, u:u + 1], y_half_v[:, u:u + 1]).then_inc(S["y_step"], 1)

            def square_y(g, u, n):
                dve.wait_ge(S["y_step"], y_at(g, u) + 2 * n + 3)
                newton_square(y_root[:, g % 2, u:u + 1], y_half_v[:, u:u + 1],
                              y_root_t[:, u:u + 1]).then_inc(S["y_step"], 1)

            def root_y(g, u, n):
                dve.wait_ge(S["y_step"], y_at(g, u) + 2 * n + 4)
                newton_root(y_root[:, g % 2, u:u + 1], y_root_t[:, u:u + 1]).then_inc(S["y_step"], 1)

            def finish_y(g, u):
                dve.wait_ge(S["y_step"], y_at(g, u) + 9)
                dve.scalar_tensor_tensor(out=y_nmr[:, g % 2, u:u + 1], in0=y_mv[:, u, 0:1], scalar=-1.0,
                                         in1=y_root[:, g % 2, u:u + 1], op0=ALU.mult,
                                         op1=ALU.mult).then_inc(S["ystat_ready"], 1)

            def shift_h(g, u, b):
                dve.wait_ge(S["mul_ready"], 2 * g + u + 1)
                y = y_sb[:, g % 2, u, :]
                dve.tensor_tensor(y, y, batch_row(ADD, b), ALU.add).then_inc(S["h_ready"], 1)

            def silu_h(g, u):
                dve.wait_ge(S["tanh_ready"], 2 * g + u + 1)
                y = y_sb[:, g % 2, u, :]
                dve.scalar_tensor_tensor(out=y, in0=t_sb[:, u, :], scalar=1.0, in1=y, op0=ALU.add,
                                         op1=ALU.mult).then_inc(S["s_ready"], 1)

            def low_s(g, u, b):
                dve.wait_ge(S["sh_ready"], 2 * g + u + 1)
                dve.scalar_tensor_tensor(out=sT[:, 1, u, :, :].rearrange("p j c -> p (j c)"), in0=ps[:, ST_BANK, :],
                                         scalar=top_r[:, 3 + b:4 + b],
                                         in1=sT[:, 0, u, :, :].rearrange("p j c -> p (j c)"), op0=ALU.mult,
                                         op1=ALU.subtract).then_inc(S["sl_ready"], 1)

            def finish_out(g, u, b):
                dve.wait_ge(S["o_done"], 2 * g + u + 1)
                dve.wait_ge(S["stored"], 16 * g - 16)
                dve.scalar_tensor_tensor(out=fo[:, g % 2, u, :], in0=ps[:, OUT_BANK, :], scalar=inv_o[:, b:b + 1],
                                         in1=batch_row(GATE, b), op0=ALU.mult,
                                         op1=ALU.mult).then_inc(S["last_gated"], 1)
                dve.wait_ge(S["last_gated"], 1)
                dve.wait_ge(S["xg_ready"], 2 * g + u + 1)
                dve.tensor_tensor(fo[:, g % 2, u, :], fo[:, g % 2, u, :], xr[:, g % 4, u, :],
                                  ALU.add).then_inc(S["last_ready"], 1)

            done = [0]

            def link(ins):
                done[0] += 1
                ins.then_inc(S["setup_step"], 1)
                dve.wait_ge(S["setup_step"], done[0])

            front(0)
            dve.wait_ge(S["prm_T"], 1)
            dve.tensor_copy(cols[:, :], ps[:, 7, 0:NR]).then_inc(S["cols_ready"], 1)
            dve.wait_ge(S["cols_ready"], 1)
            dve.wait_ge(S["silu_ready"], 1)
            dve.scalar_tensor_tensor(out=silu2[:, :], in0=silu_t[:, :], scalar=1.0, in1=cols[:, 2 * C:NR],
                                     op0=ALU.add, op1=ALU.mult).then_inc(S["silu2_ready"], 1)

            def size_weight(n, raw, came, scaled):
                dve.wait_ge(came, 16)
                link(dve.tensor_reduce(size_c[:, :], raw, AX.X, ALU.max, apply_absolute_value=True))
                if scaled:
                    link(dve.tensor_tensor(size_c[:, :], size_c[:, :], cols[:, 0:C], ALU.mult))
                dve.tensor_reduce(stat[:, n:n + 1], size_c[:, :], AX.X, ALU.max,
                                  apply_absolute_value=True).then_inc(S["stat_ready"], 1)

            def size_all(n):
                dve.wait_ge(S["statT"], n + 1)
                dve.tensor_reduce(stat_m[:, :], ps[0:1, 7, 0:P], AX.X, ALU.max).then_inc(S["stat_max_done"], 1)

            def to_power(src, a, z):
                link(dve.tensor_scalar(pow2[:, a:z], src, 1e-30, None, ALU.max))
                link(dve.tensor_scalar(pow2[:, a:z].bitcast(I32), pow2[:, a:z].bitcast(I32), EXPONENT, None,
                                       ALU.bitwise_and))
                link(dve.reciprocal(top_r[:, a:z], pow2[:, a:z]))
                link(dve.tensor_scalar(top_r[:, a:z], top_r[:, a:z], TOP, None, ALU.mult))

            def scale_weight(n, inv):
                dve.wait_ge(S["stat_b"], n + 1)
                to_power(ps[:, 7, P:P + 1], n, n + 1)
                if inv is not None:
                    link(dve.tensor_scalar(norm_top[:, n, :], cols[:, 0:C], top_r[:, n:n + 1], None, ALU.mult))
                    link(dve.tensor_scalar(inv[:, :], pow2[:, n:n + 1], 1.0 / (TOP * Z_SCALE), None, ALU.mult))
                dve.memset(spot[:, 0, 0:1], 0.0).then_inc(S["scales_ready"], 1)

            size_weight(0, wk_raw, S["wk_in"], True)
            stats_x(1, 0)
            size_all(0)
            stats_x(1, 1)
            scale_weight(0, inv_k)
            aggregate_x(1)
            halve_x(1)
            guess_x(1)
            for j in range(C):
                dve.wait_ge(S["wk_hi"], j + 1)
                last = dve.scalar_tensor_tensor(out=wk[:, 1, j, :], in0=wk_raw[:, j, :],
                                                scalar=norm_top[:, 0, j:j + 1], in1=wk[:, 0, j, :], op0=ALU.mult,
                                                op1=ALU.subtract)
                if 0 < j < C:
                    square_x(1, j - 1)
                    root_x(1, j - 1)
            last.then_inc(S["wk_ready"], 1)
            finish_x(1)
            for n in range(2, 5):
                front(n)
            dve.wait_ge(S["bias_ready"], 1)

            def bound_silu():
                dve.wait_ge(S["row_step"], 6)
                link(dve.tensor_reduce(bound[:, :], wide[0:B, SNG:SNB + 1, :], AX.X, ALU.max,
                                       apply_absolute_value=True))
                link(dve.scalar_tensor_tensor(out=bound[:, 0:1], in0=bound[:, 0:1], scalar=math.sqrt(D) * 1.01,
                                              in1=bound[:, 1:2], op0=ALU.mult, op1=ALU.add))
                dve.tensor_scalar(bound_d[:, :], ident[0:B, 0:B], bound[:, 0:1], None,
                                  ALU.mult).then_inc(S["bound_diag"], 1)

            def scale_silu():
                dve.wait_ge(S["bound_b"], 1)
                to_power(ps[:, 7, P:P + B], 3, 3 + B)
                for b in range(B):
                    link(dve.scalar_tensor_tensor(out=inv_o[:, b:b + 1], in0=pow2[:, 3 + b:4 + b],
                                                  scalar=0.5 / TOP ** 2, in1=pow2[:, 2:3], op0=ALU.mult,
                                                  op1=ALU.mult))
                dve.memset(spot[:, 1, 0:1], 0.0).then_inc(S["scales_ready"], 1)

            for b in range(B):
                first = b * NP
                dve.wait_ge(S["acc_cleared"], 2 * b + 1)

                if b > 0:
                    for u in range(2):
                        stats_x(first + 4, u)
                for i in range(NP):
                    g = first + i
                    roots, comes = (b > 0 or i > 0) and i + 4 < NP, i + 5 < NP
                    ends = i + 3 < NP and i > (0 if b > 0 else 2)
                    if ends:
                        square_x(g + 3, 2)
                    if b > 0 and i == 1:
                        dve.wait_ge(S["o_done"], 2 * first)
                    if b > 0 and i == 2:
                        dve.wait_ge(S["stored"], 16 * first)
                    keep_k(g, i, 0)
                    if ends:
                        root_x(g + 3, 2)
                    keep_k(g, i, 1)
                    if ends:
                        finish_x(g + 3)
                    if roots:
                        aggregate_x(g + 4)
                    running_max(g, i, 0)
                    if roots:
                        halve_x(g + 4)
                    running_max(g, i, 1)
                    if roots:
                        guess_x(g + 4)
                    if comes:
                        stats_x(g + 5, 0)
                    if roots:
                        square_x(g + 4, 0)
                    if comes:
                        stats_x(g + 5, 1)
                    if roots:
                        root_x(g + 4, 0)
                        square_x(g + 4, 1)
                        root_x(g + 4, 1)
                    if b == 0 and i == 1:
                        square_x(g + 4, 2)
                        root_x(g + 4, 2)
                        finish_x(g + 4)
                dve.wait_ge(S["kT_done"], b + 1)
                dve.tensor_reduce(m_col[:, :], ps[:, M_BANK:M_BANK + 2, :].rearrange("p u (j t) -> p j u t", j=C),
                                  AX.XY, ALU.max).then_inc(S["ctx_step"], 1)
                dve.wait_ge(S["ctx_step"], 6 * b + 1)
                dve.tensor_tensor(m_diag[:, :, :],
                                  ident[:, :].rearrange("p (o c) -> p o c", o=1).broadcast_to([P, C, P]),
                                  m_col[:, :].rearrange("p (j o) -> p j o", o=1).broadcast_to([P, C, P]),
                                  ALU.mult).then_inc(S["mdiag_ready"], 1)
                dve.wait_ge(S["mrow_done"], b + 1)
                if b > 0:
                    dve.wait_ge(S["ctx_done"], b)
                else:
                    dve.wait_ge(S["emb_done"], 2)
                dve.scalar_tensor_tensor(out=ek[:, first % 2, 0, :], in0=ps[:, M_BANK, :], scalar=EK_SHIFT,
                                         in1=k_all[:, 0, 0, :], op0=ALU.subtract,
                                         op1=ALU.subtract).then_inc(S["ksub_first"], 1)
                dve.tensor_scalar(m_row, ps[:, M_BANK, :], EK_SHIFT, None, ALU.subtract).then_inc(S["mrow_ready"], 1)
                dve.wait_ge(S["acc_cleared"], 2 * b + 2)
                dve.wait_ge(S["ekh_first"], b + 1)
                dve.tensor_tensor(ekl[:, first % 2, 0, :], ek[:, first % 2, 0, :], ekh[:, first % 2, 0, :],
                                  ALU.subtract).then_inc(S["ekl_first"], 1)
                dve.wait_ge(S["ekh_ready"], first + 1)
                dve.tensor_tensor(ekl[:, first % 2, 1, :], ek[:, first % 2, 1, :], ekh[:, first % 2, 1, :],
                                  ALU.subtract).then_inc(S["ekl_ready"], 1)
                dve.tensor_tensor(acc[:, :, :], acc[:, :, :], ek[:, first % 2, :, :], ALU.add).then_inc(S["s_done"], 1)
                split_ek(first + 1)
                if b + 1 < B:
                    for i in range(2, NP):
                        split_ek(first + i)
                        if i in (3, 5):
                            front(first + NP + i // 2 - 1)
                        if i == 2:
                            size_weight(1, wq_raw, S["wq_in"], True)
                        elif i == 3:
                            size_all(1)
                        elif i == 4:
                            scale_weight(1, inv_q)
                            size_weight(2, wo_raw, S["wo_in"], False)
                        elif i == 5:
                            size_all(2)
                        elif i == 6:
                            scale_weight(2, None)
                            bound_silu()
                    scale_silu()
                else:
                    with dve.Fori(2, NP) as i:
                        split_ek(i + first)
                if b == 0:
                    dve.wait_ge(S["bias_ready"], 3)
                for u in range(first_q[b]):
                    keep_q(first, u)
                    max_q(first, u)
                dve.wait_ge(S["g_pair"], first + NP)
                dve.wait_ge(S["s_done"], first + NP)
                dve.tensor_copy(gT[:, 2:4, :], ps[:, G_BANK + 2:G_BANK + 4, :]).then_inc(S["gT_ready"], 1)

                def start_q(t):
                    keep_q(first + t // 2, t % 2)
                    max_q(first + t // 2, t % 2)

                start_q(0 if b == 0 else 2)
                dve.wait_ge(S["s_sum"], b + 1)
                dve.reciprocal(r_s[:, :], ps[:, CTX_BANK + 1, 0:C]).then_inc(S["ctx_step"], 1)
                dve.wait_ge(S["ctx_step"], 6 * b + 2)
                dve.wait_ge(S["bd_cleared"], 2 + HC)
                dve.wait_ge(S["ctx_done"], b + 1)
                for r in range(HC):
                    q = slice(r * DH, (r + 1) * DH)
                    last = dve.tensor_tensor(
                        ctx_bd[q, :, r, 0:DH], ps[q, CTX_BANK, :].rearrange("p (j c) -> p j c", j=C)[:, :, q],
                        r_s[q, :].rearrange("p (j o) -> p j o", o=1).broadcast_to([DH, C, DH]), ALU.mult)
                    last.then_inc(S["ctx_step"], 1)
                dve.wait_ge(S["ctx_step"], 6 * b + 6)
                for r in range(HC):
                    q = slice(r * DH, (r + 1) * DH)
                    last = dve.tensor_tensor(
                        ctx_bd[q, :, r, 0:DH], ctx_bd[q, :, r, 0:DH],
                        vb_row[q, :].rearrange("p (j c) -> p j c", j=C)[:, :, q], ALU.add)
                    last.then_inc(S["ctx_ready"], 1)

                def step(i, g, u):
                    i1, g1, u1 = ahead(i, g, u, 1)
                    i2, g2, u2 = ahead(i, g, u, 2)
                    i3, g3, u3 = ahead(i, g, u, 3)
                    i5, g5, u5 = ahead(i, g, u, 5)
                    i0, g0, u0 = ahead(i, g, u, -1)
                    roots = lives(i2)
                    more_q = lives(i5) and not (isinstance(i5, int) and i5 < 2)
                    early = isinstance(i, int) and 2 * i + u <= 0
                    if lives(i1):
                        finish_y(g1, u1)
                    if roots:
                        aggregate_y(g2, u2)
                    if lives(i0):
                        low_s(g0, u0, b)
                    if roots:
                        halve_y(g2, u2)
                    if more_q:
                        keep_q(g5, u5)
                    if roots:
                        guess_y(g2, u2)
                    if lives(i3) and early:
                        invert_sum(g3, u3)
                        keep_y(g3, u3)
                    if more_q and early:
                        max_q(g5, u5)
                    if lives(i1):
                        shift_h(g1, u1, b)
                    if roots:
                        square_y(g2, u2, 0)
                    if more_q and not early:
                        max_q(g5, u5)
                    if roots:
                        root_y(g2, u2, 0)
                    if lives(i3) and not early:
                        invert_sum(g3, u3)
                    if roots:
                        square_y(g2, u2, 1)
                    if lives(i3) and not early:
                        keep_y(g3, u3)
                    if roots:
                        root_y(g2, u2, 1)
                    if lives(i1):
                        silu_h(g1, u1)
                    if roots:
                        square_y(g2, u2, 2)
                    if lives(i3):
                        stats_y(g3, u3)
                    if roots:
                        root_y(g2, u2, 2)

                start_q(1 if b == 0 else 3)
                step(-2, first - 2, 1)
                if b == 0:
                    start_q(2)
                    start_q(3)
                step(-1, first - 1, 0)
                over_tiles(dve, b, 2, step)
                for i in range(NP - 3, NP):
                    for u in range(2):
                        step(i, first + i, u)
                        if i == NP - 1 and b + 1 < B:
                            if u == 0:
                                front_start(first + NP + 2)
                            else:
                                front_end(first + NP + 2)
                low_s(first + NP - 1, 1, b)
                if b + 1 < B:
                    front(first + NP + 3)
                else:
                    finish_out(first + NP - 1, 1, b)

        @block.tensor
        def _(pe):
            def three(out_ap, high, low, w, ready=None):
                n = 0
                for s, part in ((0, high), (1, high), (0, low)):
                    for j in range(C):
                        last = pe.matmul(out_ap, part(j), w[:, s, j, :], start=(n == 0), stop=(n == 3 * C - 1))
                        n += 1
                last.then_inc(ready, 1)

            def turn_z(g, i):
                pe.wait_ge(S["zl_ready"], g + 1)
                for u in range(2):
                    for s, z in enumerate((zh, zl)):
                        for j in range(C):
                            last = pe.transpose(ps16[:, Q_BANK + u, (s * C + j) * P:(s * C + j + 1) * P],
                                                z[:, 2 * i + u, j * P:(j + 1) * P], ident16[:, :])
                    last.then_inc(S["t_done"], 1)

            def product_k(g, i, u):
                pe.wait_ge(S["zT_ready"], 2 * g + u + 1)
                if not starts(g, 2):
                    pe.wait_ge(S["k_ready"], 2 * g + u - 3)
                bank = K_BANK + 2 * (g % 2) + u
                three(ps[:, bank, :], lambda j: zT[:, 2 * i + u, 0, j, :], lambda j: zT[:, 2 * i + u, 1, j, :], wk,
                      S["k_done"])

            def product_q(g, i, u):
                if not starts(g, 1):
                    pe.wait_ge(S["q_evac"], 2 * g + u - 1)
                three(ps[:, Q_BANK + u, :], lambda j: zT[:, 2 * i + u, 0, j, :], lambda j: zT[:, 2 * i + u, 1, j, :],
                      wq, S["q_done"])

            def product_g(g, i, start, stop):
                for u in range(2):
                    if not (start and u == 0):
                        pe.wait_ge(S["ekl_ready"], g + 1)
                    for c in range(C):
                        for n, (z, e) in enumerate(((zh, ekh), (zh, ekl), (zl, ekh))):
                            last = pe.matmul(ps[:, G_BANK + c, :], z[:, 2 * i + u, c * P:(c + 1) * P],
                                             e[:, g % 2, u, :], start=start and u == 0 and n == 0,
                                             stop=stop and u == 1 and n == 2)
                last.then_inc(S["g_pair"], 1)
                return last

            def turn_q(g, a, u):
                pe.wait_ge(S["qexp_done"], 2 * g + u + 1)
                if not starts(g, 1):
                    pe.wait_ge(S["eqT_ready"], 2 * g + u - 1)
                for j in range(C):
                    last = pe.transpose(ps[:, EQT_BANK + u, j * P:(j + 1) * P], q_sb[:, a, u, j * P:(j + 1) * P],
                                        ident[:, :])
                last.then_inc(S["eqT_done"], 1)

            def product_y(g, u):
                pe.wait_ge(S["eqT_ready"], 2 * g + u + 1)
                if not (starts(g, 1) and u == 0):
                    pe.wait_ge(S["y_ready"], 2 * g + u)
                for j in range(C):
                    last = pe.matmul(ps[:, Y_BANK + j // 2, (j % 2) * YW:(j % 2 + 1) * YW], eqT[:, u, j, :],
                                     ctx_bd[:, j, :, :].rearrange("p h d -> p (h d)"), start=True, stop=True)
                last.then_inc(S["y_done"], 1)

            def turn_s(g, a, u):
                pe.wait_ge(S["s_ready"], 2 * g + u + 1)
                if not (starts(g, 1) and u == 0):
                    pe.wait_ge(S["sl_ready"], 2 * g + u)
                for j in range(C):
                    last = pe.transpose(ps[:, ST_BANK, j * P:(j + 1) * P], y_sb[:, a, u, j * P:(j + 1) * P],
                                        ident[:, :])
                last.then_inc(S["sT_done"], 1)

            def product_out(g, u):
                pe.wait_ge(S["sl_ready"], 2 * g + u + 1)
                if not (starts(g, 1) and u == 0):
                    pe.wait_ge(S["fin_ready"], 2 * g + u)
                three(ps[:, OUT_BANK, :], lambda j: sT[:, 0, u, j, :], lambda j: sT[:, 1, u, j, :], wo, S["o_done"])

            def turn_size(n):
                pe.wait_ge(S["stat_ready"], n + 1)
                pe.transpose(ps[0:1, 7, 0:P], stat[:, n:n + 1], ident[:, :]).then_inc(S["statT"], 1)

            def spread_size(n):
                pe.wait_ge(S["stat_max_done"], n + 1)
                pe.matmul(ps[:, 7, P:P + 1], ones[0:1, :], stat_m[:, :], start=True, stop=True).then_inc(S["stat_b"], 1)

            def bias_terms(w, bank, a, z):
                for j in range(a, z):
                    pe.matmul(ps[:, bank, :], cols[:, C + j:C + j + 1].broadcast_to([P, P]), w[:, j, :],
                              start=(j == 0), stop=False)

            def add_bias(n, bank):
                pe.matmul(ps[:, bank, :], ones[0:1, :], wide[0:1, n, :], start=False,
                          stop=True).then_inc(S["bias_done"], 1)

            def modulation_product(h):
                for j in range(C):
                    e = emb_front if j < 2 else emb_back
                    last = pe.matmul(ps[0:B, K_BANK + h, :], silu2[:, j:B * C:C],
                                     e[:, j % 2, h * D:(h + 1) * D], start=(j == 0), stop=(j == C - 1))
                last.then_inc(S["emb_done"], 1)

            pe.wait_ge(S["const_ready"], 4)
            pe.wait_ge(S["prm_in"], 48)
            pe.transpose(ps[:, 7, 0:NR], prm[:, :], ident[0:NR, 0:NR]).then_inc(S["prm_T"], 1)
            pe.wait_ge(S["cols_ready"], 1)
            pe.wait_ge(S["wk_in"], 16)
            pe.wait_ge(S["bias_in"], 48)
            turn_size(0)
            spread_size(0)
            turn_z(0, 0)
            bias_terms(wk_raw, 6, 0, C - 1)
            pe.wait_ge(S["wk_ready"], 1)
            product_k(0, 0, 0)
            bias_terms(wk_raw, 6, C - 1, C)
            add_bias(0, 6)
            pe.wait_ge(S["zT_ready"], 2)
            turn_z(1, 1)
            product_k(0, 0, 1)

            for b in range(B):
                first = b * NP

                def step_a(i, g, more=True):
                    product_k(g, i, 0)
                    if more:
                        pe.wait_ge(S["zT_ready"], 2 * g + 2)
                        turn_z(g + 1, i + 1)
                    product_k(g, i, 1)

                if b == 0:
                    step_a(1, 1)
                    with pe.Fori(2, NP - 1) as i:
                        step_a(i, i)
                else:
                    pe.wait_ge(S["zT_ready"], 2 * (first + 2))
                    turn_z(first + 2, 2)
                    with pe.Fori(2, NP - 1) as i:
                        step_a(i, i + first)
                step_a(NP - 1, first + NP - 1, False)
                pe.wait_ge(S["zT_ready"], 2 * (first + NP))
                if b == 0:
                    pe.wait_ge(S["silu2_ready"], 1)
                    pe.wait_ge(S["emb_in"], 32)
                    pe.wait_ge(S["k_ready"], 2 * NP - 2)
                    modulation_product(0)
                else:
                    product_q(first, 0, 0)
                pe.wait_ge(S["kmax_done"], 2 * (first + NP))
                for u in range(2):
                    for j in range(C):
                        last = pe.transpose(ps[:, M_BANK + u, j * P:(j + 1) * P], acc[:, u, j * P:(j + 1) * P],
                                            ident[:, :])
                last.then_inc(S["kT_done"], 1)
                if b > 0:
                    product_q(first, 0, 1)
                else:
                    modulation_product(1)
                pe.wait_ge(S["mdiag_ready"], b + 1)
                pe.matmul(ps[:, M_BANK, :], ones[:, :], m_diag[:, :, :].rearrange("p j c -> p (j c)"), start=True,
                          stop=True).then_inc(S["mrow_done"], 1)
                if b == 0:
                    pe.wait_ge(S["wv_in"], 16)
                    bias_terms(wv, 7, 0, C)
                    add_bias(2, 7)
                pe.wait_ge(S["k_ready"], 2 * (first + NP))
                if b == 0:
                    pe.wait_ge(S["emb_kept"], 1)
                pe.wait_ge(S["ekl_first"], b + 1)
                product_g(first, 0, True, False)
                if b == 0:
                    for i in range(1, NP - 1):
                        product_g(i, i, False, False)
                        if i == 2:
                            pe.wait_ge(S["bias_ready"], 2)
                            turn_size(1)
                        elif i == 3:
                            spread_size(1)
                            bias_terms(wq_raw, 6, 0, C)
                            add_bias(1, 6)
                        elif i == 4:
                            turn_size(2)
                        elif i == 5:
                            spread_size(2)
                else:
                    with pe.Fori(1, NP - 1) as i:
                        product_g(i + first, i, False, False)
                product_g(first + NP - 1, NP - 1, False, True)
                if b == 0:
                    pe.wait_ge(S["bound_diag"], 1)
                    pe.matmul(ps[:, 7, P:P + B], ones[0:B, :], bound_d[:, :], start=True,
                              stop=True).then_inc(S["bound_b"], 1)
                    pe.wait_ge(S["w_ready"], 1)
                    product_q(first, 0, 0)
                else:
                    product_q(first + 1, 1, 0)
                pe.wait_ge(S["s_done"], first + NP)
                pe.wait_ge(S["scales_ready"], 4)
                for j in range(C):
                    for u in range(2):
                        last = pe.matmul(ps[:, CTX_BANK + 1, j:j + 1], acc[:, u, j * P:(j + 1) * P], z256[:, :],
                                         start=(u == 0), stop=(u == 1))
                last.then_inc(S["s_sum"], 1)
                pe.wait_ge(S["gT_ready"], 2 * b + 2)
                pe.wait_ge(S["wv_ready"], C)
                for j in range(C):
                    for c in range(C):
                        last = pe.matmul(ps[:, CTX_BANK, j * P:(j + 1) * P], gT[:, c, j * P:(j + 1) * P],
                                         wv[:, c, j * P:(j + 1) * P], start=(c == 0), stop=(c == C - 1))
                last.then_inc(S["ctx_done"], 1)
                turn_q(first, 0, 0)
                if b == 0:
                    product_q(first, 0, 1)
                else:
                    turn_q(first, 0, 1)
                    product_q(first + 1, 1, 1)
                pe.wait_ge(S["ctx_ready"], HC * (b + 1))
                product_y(first, 0)
                if b == 0:
                    product_q(first + 1, 1, 0)
                    turn_q(first, 0, 1)
                    product_q(first + 1, 1, 1)
                else:
                    product_q(first + 2, 2, 0)
                product_y(first, 1)
                turn_q(first + 1, 1, 0)
                if b == 0:
                    product_q(first + 2, 2, 0)
                product_y(first + 1, 0)
                if b == 0:
                    pe.wait_ge(S["w_ready"], 2)

                def step_c(i, g, a, u):
                    i3, g3, u3 = ahead(i, g, u, 3)
                    i5, g5, u5 = ahead(i, g, u, 5)
                    a3 = (a + (u + 3) // 2) % 2
                    i0, g0, u0 = ahead(i, g, u, -1)
                    if lives(i3):
                        turn_q(g3, a3, u3)
                    if lives(i5):
                        product_q(g5, i5, u5)
                    late = isinstance(i, int) and 2 * i + u == 0
                    if lives(i) and not late:
                        turn_s(g, a, u)
                    if lives(i3):
                        product_y(g3, u3)
                    if late:
                        turn_s(g, a, u)
                    if lives(i0):
                        product_out(g0, u0)

                for u in range(2):
                    step_c(0, first, 0, u)
                with pe.Fori(0, (NP - 4) // 2) as n:
                    for p in range(2):
                        for u in range(2):
                            step_c(n * 2 + (1 + p), n * 2 + (first + 1 + p), 1 - p, u)
                for i in range(NP - 3, NP + 1):
                    for u in range(2):
                        step_c(i, first + i, i % 2, u)
                        if b + 1 < B:
                            nxt = first + NP
                            if (i, u) == (NP - 3, 1):
                                pe.wait_ge(S["q_evac"], 2 * nxt)
                                turn_z(nxt, 0)
                            elif (i, u) == (NP - 2, 0):
                                pe.wait_ge(S["eqT_ready"], 2 * nxt - 1)
                                product_k(nxt, 0, 0)
                            elif (i, u) == (NP - 2, 1):
                                pe.wait_ge(S["eqT_ready"], 2 * nxt)
                                product_k(nxt, 0, 1)
                                pe.wait_ge(S["zT_ready"], 2 * nxt + 2)
                                turn_z(nxt + 1, 1)
                            elif i == NP - 1:
                                pe.wait_ge(S["y_ready"], 2 * nxt)
                                product_k(nxt + 1, 1, u)


_INS = ["x", "cond_1024"] + ["L0_cond_" + n for n in (
    "norm_g", "norm_b", "Wq", "bq", "Wk", "bk", "Wv", "bv", "emb_W", "emb_b", "sn_g", "sn_b", "out_W", "out_b")]


def kernel(**inputs):
    import numpy as np
    from concourse import bacc
    from concourse.bass_utils import run_bass_kernel_spmd

    nc = bacc.Bacc("TRN2", target_bir_lowering=False, num_devices=1)
    arrays, args = {}, []
    for name in _INS:
        a = np.ascontiguousarray(inputs[name])
        arrays[f"in_{name}_dram"] = a
        args.append(nc.dram_tensor(f"in_{name}_dram", a.shape, mybir.dt.from_np(a.dtype), kind="ExternalInput").ap())
    shape = arrays["in_x_dram"].shape
    args.append(nc.dram_tensor("out_0_dram", shape, F32, kind="ExternalOutput").ap())
    linear_attention_block(nc, *args)
    r = run_bass_kernel_spmd(nc, [arrays], core_ids=[0])
    return r.results[0]["out_0_dram"]
```
